# Optimizing a Trainium2 kernel written in Bass

```python
import numpy as np
import jax
import jax.numpy as jnp

def _softmax(x, axis=-1):
    return jax.nn.softmax(x, axis=axis)

def _gelu(x):
    return jax.nn.gelu(x, approximate=True)

def _silu(x):
    return jax.nn.silu(x)

def _sigmoid(x):
    return jax.nn.sigmoid(x)

def _layernorm(x, axis=-1, eps=1e-05):
    m = jnp.mean(x, axis=axis, keepdims=True)
    v = jnp.var(x, axis=axis, keepdims=True)
    return (x - m) / jnp.sqrt(v + eps)

def _scatter_add(tgt, idx, src, axis=0):
    return tgt.at[idx].add(src)

def _segment_sum(src, seg, n):
    return jax.ops.segment_sum(src, seg, n)
kernel_name = 'mk_adaln_ffn_d2_seqx_r4_6f1d1e'

def setup_inputs(seed: int=0):
    np.random.seed(seed)
    _w = jnp.asarray

    def _rec_inputs():
        import jax
        import jax.numpy as jnp
        _rk = jax.random.key(seed)
        x = 7.22e-05 + 1 * jax.random.normal(jax.random.fold_in(_rk, 1), (8, 256, 512), jnp.float32)
        _lenS = 256 - jax.random.randint(jax.random.fold_in(_rk, 7), (8,), 0, max(1, 256 // 4) + 1, jnp.int32)
        _lenS2 = 256 - jax.random.randint(jax.random.fold_in(_rk, 8), (8,), 0, max(1, 256 // 4) + 1, jnp.int32)
        cond_2048 = jax.random.bernoulli(jax.random.fold_in(_rk, 11), 0.5063, (8, 512)).astype(jnp.float32)
        return (x, cond_2048)
    x, cond_2048 = _rec_inputs()

    def _L0_cond_setup():
        import jax, jax.numpy as jnp
        import numpy as np
        NH = 8
        NEG = -1e+30
        key = jax.random.key(seed)
        k1, k2, k3, k4 = jax.random.split(key, 4)
        B, D, T = (4, 256, 512)
        x = jax.random.normal(k1, (B, D, T), dtype=jnp.float32)
        mask = jax.random.randint(k2, (B, T), 0, 2).astype(jnp.float32)
        lim = float(np.sqrt(6.0 / (D + D)))
        Wq = jax.random.uniform(k3, (D, D), dtype=jnp.float32, minval=-lim, maxval=lim)
        Wo = jax.random.uniform(k4, (D, D), dtype=jnp.float32, minval=-lim, maxval=lim)
        return {'x': x, 'mask': mask, 'Wq': Wq, 'Wo': Wo}
    _L0_cond_all = _L0_cond_setup()
    _L0_cond_in = {k: v for k, v in _L0_cond_all.items() if k in ('Wq', 'Wo')}
    del _L0_cond_all

    def _L0_ffn_setup():
        import jax, jax.numpy as jnp
        import numpy as np
        B, S, H, F, E, K = (4, 512, 512, 352, 8, 2)
        key = jax.random.key(seed)
        k0, k1, k2, k3, k4 = jax.random.split(key, 5)
        return {'hidden_states': jax.random.normal(k0, (B, S, H), dtype=jnp.float32), 'w_router': jax.random.normal(k1, (H, E), dtype=jnp.float32) * (1.0 / np.sqrt(H)), 'w_gate': jax.random.normal(k2, (E, H, F), dtype=jnp.float32) * (1.0 / np.sqrt(H)), 'w_up': jax.random.normal(k3, (E, H, F), dtype=jnp.float32) * (1.0 / np.sqrt(H)), 'w_down': jax.random.normal(k4, (E, F, H), dtype=jnp.float32) * (1.0 / np.sqrt(F))}
    _L0_ffn_all = _L0_ffn_setup()
    _L0_ffn_in = {k: v for k, v in _L0_ffn_all.items() if k in ('w_router', 'w_gate', 'w_up', 'w_down')}
    del _L0_ffn_all

    def _L1_cond_setup():
        import jax, jax.numpy as jnp
        import numpy as np
        HEADS = 16
        EPS = 1e-06

        def _rms_norm(x, g):
            xf = x.astype(jnp.float32)
            y = xf * jax.lax.rsqrt(jnp.mean(xf * xf, axis=-1, keepdims=True) + EPS)
            return y.astype(x.dtype) * g
        key = jax.random.key(seed)
        ks = jax.random.split(key, 6)
        b, n, dim, emb_dim = (4, 512, 512, 512)
        d_head = dim // HEADS
        return {'x': jax.random.normal(ks[0], (b, n, dim), jnp.float32), 'emb': jax.random.normal(ks[1], (b, 1, emb_dim), jnp.float32), 'W_emb': jax.random.normal(ks[2], (emb_dim, 2 * dim), jnp.float32) * emb_dim ** (-0.5), 'b_emb': jnp.zeros((2 * dim,), jnp.float32), 'g_norm': jnp.ones((dim,), jnp.float32), 'W_qkv': jax.random.normal(ks[3], (dim, 3 * dim), jnp.float32) * dim ** (-0.5), 'g_q': jnp.ones((d_head,), jnp.float32), 'g_k': jnp.ones((d_head,), jnp.float32), 'W_out': jax.random.normal(ks[4], (dim, dim), jnp.float32) * dim ** (-0.5)}
    _L1_cond_all = _L1_cond_setup()
    _L1_cond_in = {k: v for k, v in _L1_cond_all.items() if k in ('W_emb', 'b_emb', 'g_norm', 'W_qkv', 'g_q', 'g_k', 'W_out')}
    del _L1_cond_all

    def _L1_ffn_setup():
        import jax, jax.numpy as jnp
        import numpy as np
        B, S, D = (4, 512, 512)
        DFF = 1408
        E, K, R = (8, 2, 16)
        SCALING = 32.0 / 16.0
        key = jax.random.key(seed)
        ks = jax.random.split(key, 12)
        s = lambda k, shape, scale: jax.random.normal(k, shape, dtype=jnp.float32) * scale
        return {'x': s(ks[0], (B, S, D), 1.0), 'Wg': s(ks[1], (DFF, D), 0.02), 'Wu': s(ks[2], (DFF, D), 0.02), 'Wd': s(ks[3], (D, DFF), 0.02), 'Wr': s(ks[4], (E, D), 0.02), 'Ag': s(ks[5], (E, R, D), 0.02), 'Bg': s(ks[6], (E, DFF, R), 0.02), 'Au': s(ks[7], (E, R, D), 0.02), 'Bu': s(ks[8], (E, DFF, R), 0.02), 'Ad': s(ks[9], (E, R, DFF), 0.02), 'Bd': s(ks[10], (E, D, R), 0.02)}
    _L1_ffn_all = _L1_ffn_setup()
    _L1_ffn_in = {k: v for k, v in _L1_ffn_all.items() if k in ('Wg', 'Wu', 'Wd', 'Wr', 'Ag', 'Bg', 'Au', 'Bu', 'Ad', 'Bd')}
    del _L1_ffn_all
    return {'x': x, 'cond_2048': cond_2048, 'L0_cond_Wq': _L0_cond_in['Wq'], 'L0_cond_Wo': _L0_cond_in['Wo'], 'L0_ffn_w_router': _L0_ffn_in['w_router'], 'L0_ffn_w_gate': _L0_ffn_in['w_gate'], 'L0_ffn_w_up': _L0_ffn_in['w_up'], 'L0_ffn_w_down': _L0_ffn_in['w_down'], 'L1_cond_W_emb': _L1_cond_in['W_emb'], 'L1_cond_b_emb': _L1_cond_in['b_emb'], 'L1_cond_g_norm': _L1_cond_in['g_norm'], 'L1_cond_W_qkv': _L1_cond_in['W_qkv'], 'L1_cond_g_q': _L1_cond_in['g_q'], 'L1_cond_g_k': _L1_cond_in['g_k'], 'L1_cond_W_out': _L1_cond_in['W_out'], 'L1_ffn_Wg': _L1_ffn_in['Wg'], 'L1_ffn_Wu': _L1_ffn_in['Wu'], 'L1_ffn_Wd': _L1_ffn_in['Wd'], 'L1_ffn_Wr': _L1_ffn_in['Wr'], 'L1_ffn_Ag': _L1_ffn_in['Ag'], 'L1_ffn_Bg': _L1_ffn_in['Bg'], 'L1_ffn_Au': _L1_ffn_in['Au'], 'L1_ffn_Bu': _L1_ffn_in['Bu'], 'L1_ffn_Ad': _L1_ffn_in['Ad'], 'L1_ffn_Bd': _L1_ffn_in['Bd']}

def reference(x, cond_2048, L0_cond_Wq, L0_cond_Wo, L0_ffn_w_router, L0_ffn_w_gate, L0_ffn_w_up, L0_ffn_w_down, L1_cond_W_emb, L1_cond_b_emb, L1_cond_g_norm, L1_cond_W_qkv, L1_cond_g_q, L1_cond_g_k, L1_cond_W_out, L1_ffn_Wg, L1_ffn_Wu, L1_ffn_Wd, L1_ffn_Wr, L1_ffn_Ag, L1_ffn_Bg, L1_ffn_Au, L1_ffn_Bu, L1_ffn_Ad, L1_ffn_Bd):
    import jax
    import jax.numpy as jnp

    def _L0_cond_ref(x, mask, Wq, Wo):
        import jax, jax.numpy as jnp
        import numpy as np
        NH = 8
        NEG = -1e+30
        B, D, T = x.shape
        dk = D // NH
        scale = 1.0 / jnp.sqrt(jnp.asarray(dk, x.dtype))
        xt = jnp.transpose(x, (0, 2, 1))
        q = xt @ Wq.T
        qh = q.reshape(B, T, NH, dk).transpose(0, 2, 1, 3)
        scores = scale * jnp.einsum('bhqd,bhkd->bhqk', qh, qh)
        cmask = mask[:, None, None, :]
        rmask = mask[:, None, :, None]
        logits = (scores * cmask + (1.0 - cmask) * NEG) * rmask
        attn = jax.nn.softmax(logits, axis=-1)
        ctx = jnp.einsum('bhqk,bhkd->bhqd', attn, qh)
        ctx = ctx.transpose(0, 2, 1, 3).reshape(B, T, D)
        out = ctx @ Wo.T
        return jnp.transpose(out, (0, 2, 1))

    def _L0_ffn_ref(hidden_states, w_router, w_gate, w_up, w_down):
        import jax, jax.numpy as jnp
        import numpy as np
        B, S, H, F, E, K = (4, 512, 512, 352, 8, 2)
        b, s, h = hidden_states.shape
        e = w_router.shape[1]
        x = hidden_states.reshape(-1, h)
        probs = jax.nn.softmax(x @ w_router, axis=-1)
        topk_w, topk_i = jax.lax.top_k(probs, K)
        topk_w = topk_w / jnp.sum(topk_w, axis=-1, keepdims=True)
        coef = jnp.einsum('tk,tke->te', topk_w, jax.nn.one_hot(topk_i, e, dtype=topk_w.dtype))
        out = jnp.zeros_like(x)
        for ex in range(e):
            hid = jax.nn.silu(x @ w_gate[ex]) * (x @ w_up[ex])
            out = out + coef[:, ex:ex + 1] * (hid @ w_down[ex])
        return out.reshape(b, s, h)

    def _L1_cond_ref(x, emb, W_emb, b_emb, g_norm, W_qkv, g_q, g_k, W_out):
        import jax, jax.numpy as jnp
        import numpy as np
        HEADS = 16
        EPS = 1e-06

        def _rms_norm(x, g):
            xf = x.astype(jnp.float32)
            y = xf * jax.lax.rsqrt(jnp.mean(xf * xf, axis=-1, keepdims=True) + EPS)
            return y.astype(x.dtype) * g
        b, n, dim = x.shape
        h = HEADS
        d = dim // h
        scale_shift = emb @ W_emb + b_emb
        scale, shift = jnp.split(scale_shift, 2, axis=-1)
        xn = _rms_norm(x, g_norm) * (1.0 + scale) + shift
        qkv = xn @ W_qkv
        qkv = qkv.reshape(b, n, 3, h, d)
        q, k, v = jnp.moveaxis(qkv, 2, 0)
        q = jnp.swapaxes(q, 1, 2)
        k = jnp.swapaxes(k, 1, 2)
        v = jnp.swapaxes(v, 1, 2)
        q = _rms_norm(q, g_q)
        k = _rms_norm(k, g_k)
        logits = jnp.einsum('bhqd,bhkd->bhqk', q, k) * d ** (-0.5)
        attn = jax.nn.softmax(logits, axis=-1)
        o = jnp.einsum('bhqk,bhkd->bhqd', attn, v)
        o = jnp.swapaxes(o, 1, 2).reshape(b, n, dim)
        return o + o @ W_out

    def _L1_ffn_ref(x, Wg, Wu, Wd, Wr, Ag, Bg, Au, Bu, Ad, Bd):
        import jax, jax.numpy as jnp
        import numpy as np
        B, S, D = (4, 512, 512)
        DFF = 1408
        E, K, R = (8, 2, 16)
        SCALING = 32.0 / 16.0
        b, s, d = x.shape
        xf = x.reshape(-1, d)
        gate_base = xf @ Wg.T
        up_base = xf @ Wu.T
        base_out = jax.nn.silu(gate_base) * up_base @ Wd.T
        router_logits = xf @ Wr.T
        probs = jax.nn.softmax(router_logits.astype(jnp.float32), axis=-1)
        topw, topi = jax.lax.top_k(probs, K)
        topw = topw.astype(x.dtype)
        expert_w = jnp.sum(jax.nn.one_hot(topi, E, dtype=x.dtype) * topw[..., None], axis=1)

        def expert_step(acc, params):
            Ag_e, Bg_e, Au_e, Bu_e, Ad_e, Bd_e, we = params
            g_lora = xf @ Ag_e.T @ Bg_e.T * SCALING
            u_lora = xf @ Au_e.T @ Bu_e.T * SCALING
            h = jax.nn.silu(gate_base + g_lora) * (up_base + u_lora)
            d_delta = h @ Ad_e.T @ Bd_e.T * SCALING
            return (acc + d_delta * we[:, None], None)
        acc0 = jnp.zeros_like(base_out)
        acc, _ = jax.lax.scan(expert_step, acc0, (Ag, Bg, Au, Bu, Ad, Bd, expert_w.T))
        return (base_out + acc).reshape(b, s, d)
    x = x + _L0_ffn_ref(_L0_cond_ref(x, cond_2048, L0_cond_Wq, L0_cond_Wo), L0_ffn_w_router, L0_ffn_w_gate, L0_ffn_w_up, L0_ffn_w_down)
    x = x + _L1_ffn_ref(_L1_cond_ref(x, cond_2048[:, None, :], L1_cond_W_emb, L1_cond_b_emb, L1_cond_g_norm, L1_cond_W_qkv, L1_cond_g_q, L1_cond_g_k, L1_cond_W_out), L1_ffn_Wg, L1_ffn_Wu, L1_ffn_Wd, L1_ffn_Wr, L1_ffn_Ag, L1_ffn_Bg, L1_ffn_Au, L1_ffn_Bu, L1_ffn_Ad, L1_ffn_Bd)
    return x

_drawn_inputs = setup_inputs


def setup_inputs(seed=0):
    import zlib

    import numpy as np

    out = dict(_drawn_inputs(seed))
    spreads = {'L1_cond_b_emb': (0.0, 0.469),
     'L1_cond_g_norm': (1.0, 0.6),
     'L1_cond_g_q': (1.0, 0.6),
     'L1_cond_g_k': (1.0, 0.6)}
    factors = {'L1_ffn_Wr': 8.0,
     'L1_ffn_Ag': 8.0,
     'L1_ffn_Bg': 8.0,
     'L1_ffn_Au': 8.0,
     'L1_ffn_Bu': 8.0,
     'L1_ffn_Ad': 8.0,
     'L1_ffn_Bd': 8.0,
     'L1_ffn_Wd': 64.0}
    for name, (base, spread) in spreads.items():
        noise = np.random.default_rng([zlib.crc32(name.encode()), seed]).standard_normal(out[name].shape)
        drawn = base * np.exp(spread * noise) if base else spread * noise
        out[name] = jnp.asarray(drawn.astype(out[name].dtype))
    for name, factor in factors.items():
        out[name] = (out[name] * factor).astype(out[name].dtype)
    return out
```

```python
from contextlib import ExitStack

import concourse.bass as bass
from concourse import mybir

F32 = mybir.dt.float32
F32R = mybir.dt.float32r
F16 = mybir.dt.float16
ALU = mybir.AluOpType
ACT = mybir.ActivationFunctionType
AX = mybir.AxisListType.X

P = 128
NB = 8
S0 = 256
T0 = 512
KF = T0 // P
NT = NB * S0 // P
E = 8
F0 = 352
F0_TILES = [(0, 128), (128, 128), (256, 96)]
DFF = 1408
FT = DFF // P
R = 16
WS = 64.0
NEG = -1e30
BIG = 3e38


class Batch:

    def __init__(self, i, q):
        self.idx = 2 * i + q
        self.half = i + q // 2
        self.par = q % 2
        self.first = isinstance(i, int) and 2 * i + q == 0


class Uses:

    def __init__(self, base, parity):
        self.base, self.k, self.parity = base, 0, parity

    def take(self):
        idx, bank = self.base + self.k, (self.parity + self.k) % 2
        self.k += 1
        return idx, bank


class Core:

    def __init__(self, heads, n, n_pre, n_post, mask_row, lag, dt):
        self.heads, self.n = heads, n
        self.tiles = n // P
        self.kps = 512 // n
        self.sph = self.tiles // self.kps
        self.slots = heads * self.sph
        self.pairs = heads // 2
        self.groups = heads // 4
        self.k_nat = 97 if mask_row else 96
        self.k_t = self.k_nat + 1
        self.n_pre, self.n_post = n_pre, n_post
        self.lag = lag
        self.dt = dt
        self.base0 = 2 * n_pre + 1
        self.uses = 1 + n_pre + n_post

    def uses_at(self, b, q):
        return Uses(self.base0 + self.uses * b.idx, (self.base0 + self.uses * q) % 2)


def plain(ap):
    return ap.bitcast(F32) if ap.dtype == F32R else ap


class Attention:

    def __init__(self, nc, ctx, tag, core, ident):
        self.nc, self.c, self.ident = nc, core, ident
        c = core
        sb = lambda name, shape, dt: ctx.enter_context(nc.sbuf_tensor(f"{tag}_{name}", shape, dt))
        ps = lambda name: ctx.enter_context(nc.psum_tensor(f"{tag}_{name}", [P, 512], F32))
        sem = lambda name: ctx.enter_context(nc.semaphore(f"{tag}_{name}"))
        self.A = [sb(f"A{i}", [c.k_t, c.heads, c.n], c.dt) for i in range(2)]
        self.B = [sb(f"B{i}", [c.k_t, c.heads, c.n], c.dt) for i in range(2)]
        self.V = [sb(f"V{i}", [P, c.tiles, c.heads, 64], F32) for i in range(2)]
        self.EX = [sb(f"EX{i}", [P, 512], F32) for i in range(4)]
        self.CS = sb("CS", [P, c.pairs, c.n], F32)
        self.CT = sb("CT", [P, c.groups, c.n], F32)
        self.CN = sb("CN", [P, c.groups, c.n], F32)
        self.RR = sb("RR", [c.heads, c.n], F32)
        self.RV = sb("RV", [c.heads, c.n], F32)
        self.NM = sb("NM", [P, c.heads * c.tiles], F32)
        self.SR = sb("SR", [c.heads * c.tiles, P], c.dt)
        self.SEL = sb("SEL", [c.heads, c.groups, P], F32)
        self.bn = [ps(f"bn{i}") for i in range(2)]
        self.bt = [ps(f"bt{i}") for i in range(2)]
        self.bc = [ps(f"bc{i}") for i in range(2)]
        self.pp = [ps(f"pp{i}") for i in range(2)]
        self.nat_made = sem("nat_made")
        self.max_done = sem("max_done")
        self.st_made = sem("st_made")
        self.exp_done = sem("exp_done")
        self.pv_done = sem("pv_done")
        self.ctx_out = sem("ctx_out")
        self.proj_made = sem("proj_made")
        self.proj_out = sem("proj_out")
        self.shift_rows = sem("shift_rows")
        self.shift_in = sem("shift_in")
        self.split_done = sem("split_done")
        self.ab_in = sem("ab_in")
        self.v_ready = sem("v_ready")
        self.ctx_in = sem("ctx_in")
        self.recip_done = sem("recip_done")
        self.ctx_norm = sem("ctx_norm")
        self.post_done = sem("post_done")
        self.dve_step = sem("dve_step")

    AB_DMAS = 24
    CTX_DMAS = 6

    def sp_assemble(self, sp, n, qh, ql, kh, kl):
        sp.wait_ge(self.split_done, n.idx + 1)
        sp.wait_ge(self.st_made, self.c.slots * (n.idx - 1) + 1) if not n.first else None
        for j in range(4):
            for r, (a, b) in enumerate(((qh, kh), (ql, kh), (qh, kl))):
                for dst, src in ((self.A, a), (self.B, b)):
                    sp.dma_start(plain(dst[n.par][32 * r:32 * r + 32, j::4, :]),
                                 plain(src[32 * j:32 * j + 32, :, :])).then_inc(self.ab_in, 16)

    def sp_shift(self, sp, n):
        c = self.c
        sp.wait_ge(self.shift_rows, n.idx + 1)
        dst = self.A[n.par][c.k_nat:c.k_t, :, :].rearrange("p h (t j) -> p (h t) j", j=P)
        sp.dma_start(plain(dst), plain(self.SR[:, :])).then_inc(self.shift_in, 16)

    def sp_context(self, sp, n):
        c = self.c
        sp.wait_ge(self.ctx_out, c.pairs * (n.idx + 1) + 2)
        sp.wait_ge(self.post_done, n.idx + 1)
        for j in range(4):
            src = self.CS[64 * (j % 2):64 * (j % 2) + 32, j // 2::2, :]
            sp.dma_start(self.CT[32 * j:32 * j + 32, :, :], src).then_inc(self.ctx_in, 16)
        for odd in range(2):
            sp.dma_start(self.RR[odd * c.pairs:(odd + 1) * c.pairs, :],
                         self.CS[32 + 64 * odd:33 + 64 * odd, :, :]).then_inc(self.ctx_in, 16)

    def pe_take(self, pe, uses):
        idx, bank = uses.take()
        pe.wait_ge(self.proj_out, idx + 1)
        return self.pp[bank]

    def pe_nat(self, pe, n, s):
        c, nc = self.c, self.nc
        if s == 0:
            pe.wait_ge(self.ab_in, 16 * self.AB_DMAS * (n.idx + 1))
        pe.wait_ge(self.max_done, c.slots * n.idx + s + 1)
        h, t0 = s // c.sph, (s % c.sph) * c.kps
        A, B = self.A[n.par], self.B[n.par]
        for k in range(c.kps):
            mm = nc.tensor.matmul(self.bn[s % 2][:, k * c.n:(k + 1) * c.n],
                                  A[0:c.k_nat, h, (t0 + k) * P:(t0 + k + 1) * P],
                                  B[0:c.k_nat, h, :], start=True, stop=True)
        mm.then_inc(self.nat_made, 1)

    def pe_shift(self, pe, n, uses):
        c = self.c
        pe.wait_ge(self.max_done, c.slots * (n.idx + 1) + 2)
        bank = self.pe_take(pe, uses)
        self.nc.tensor.transpose(bank[0:c.heads * c.tiles, 0:P], self.NM[:, :], self.ident[:, :]).then_inc(self.proj_made, 1)

    def pe_st(self, pe, n, s):
        c, nc = self.c, self.nc
        if s == 0:
            pe.wait_ge(self.shift_in, 16 * (n.idx + 1))
        pe.wait_ge(self.exp_done, c.slots * n.idx + s + 1)
        h, t0 = s // c.sph, (s % c.sph) * c.kps
        A, B = self.A[n.par], self.B[n.par]
        for k in range(c.kps):
            mm = nc.tensor.matmul(self.bt[s % 2][:, k * c.n:(k + 1) * c.n],
                                  B[0:c.k_t, h, (t0 + k) * P:(t0 + k + 1) * P],
                                  A[0:c.k_t, h, :], start=True, stop=True)
        mm.then_inc(self.st_made, 1)

    def pe_pv(self, pe, n, s):
        c, nc = self.c, self.nc
        if s == 0:
            pe.wait_ge(self.v_ready, n.idx + 1)
        h, t0 = s // c.sph, (s % c.sph) * c.kps
        if h % 2 == 0 and t0 == 0:
            pe.wait_ge(self.ctx_out, c.pairs * n.idx + h // 2 + 1)
        pe.wait_ge(self.exp_done, c.slots * n.idx + s + 3)
        half = 64 * (h % 2)
        for k in range(c.kps):
            t = t0 + k
            mm = nc.tensor.matmul(self.bc[h // 2 % 2][half:half + 64, 0:c.n], self.V[n.par][:, t, h, :],
                                  self.EX[s % 4][:, k * c.n:(k + 1) * c.n],
                                  start=(t == 0), stop=(t == c.tiles - 1), tile_position=(0, half))
        mm.then_inc(self.pv_done, 1)

    def pe_spread(self, pe, n, uses):
        c, nc = self.c, self.nc
        pe.wait_ge(self.recip_done, n.idx + 1)
        for u in range(2):
            bank = self.pe_take(pe, uses)
            for k in range(c.kps):
                mm = nc.tensor.matmul(bank[:, k * c.n:(k + 1) * c.n], self.SEL[:, u * c.kps + k, :],
                                      self.RV[:, :], start=True, stop=True)
            mm.then_inc(self.proj_made, 1)

    def pe_slots(self, pe, b, nxt):
        c = self.c
        self.pe_st(pe, b, 0)
        self.pe_st(pe, b, 1)
        for s in range(c.slots):
            if s + 2 < c.slots:
                self.pe_st(pe, b, s + 2)
            self.pe_pv(pe, b, s)
            if nxt is not None and s >= c.lag:
                self.pe_nat(pe, nxt, s - c.lag)
        if nxt is not None:
            for s in range(c.slots - c.lag, c.slots):
                self.pe_nat(pe, nxt, s)

    def act_slots(self, act, b):
        c, nc = self.c, self.nc

        def copy_context(pr):
            if pr == 0:
                act.wait_ge(self.ctx_in, 16 * self.CTX_DMAS * b.idx + 1)
            act.wait_ge(self.pv_done, c.slots * b.idx + (pr + 1) * 2 * c.sph + 4)
            nc.scalar.copy(self.CS[:, pr, :], self.bc[pr % 2][:, 0:c.n]).then_inc(self.ctx_out, 1)

        for s in range(c.slots):
            g = c.slots * b.idx + s
            act.wait_ge(self.st_made, g + 2)
            act.wait_ge(self.pv_done, g + 1)
            nc.scalar.activation(self.EX[s % 4][:, :], self.bt[s % 2][:, :], ACT.Exp).then_inc(self.exp_done, 1)
            if s >= 2 and (s - 1) % (2 * c.sph) == 0:
                copy_context((s - 1) // (2 * c.sph) - 1)
        copy_context(c.pairs - 1)

    def dve_max(self, dve, n, s):
        c = self.c
        dve.wait_ge(self.nat_made, c.slots * n.idx + s + 1)
        cols = c.kps
        self.nc.vector.tensor_reduce(self.NM[:, s * cols:(s + 1) * cols],
                                     self.bn[s % 2][:, :].rearrange("p (k n) -> p k n", k=cols),
                                     AX, ALU.max, negate=True).then_inc(self.max_done, 1)

    def dve_wait(self, dve, uses):
        idx, bank = uses.take()
        dve.wait_ge(self.proj_made, idx + 1)
        return self.pp[bank]

    def dve_shift(self, dve, n, uses):
        c = self.c
        bank = self.dve_wait(dve, uses)
        if not n.first:
            dve.wait_ge(self.shift_in, 16 * n.idx)
        self.nc.vector.tensor_copy(self.SR[:, :], bank[0:c.heads * c.tiles, 0:P]).then_inc(self.shift_rows, 1)
        dve.wait_ge(self.shift_rows, n.idx + 1)
        dve.sem_inc(self.proj_out, 1)

    def dve_recip(self, dve, n):
        dve.wait_ge(self.ctx_in, 16 * self.CTX_DMAS * (n.idx + 1) + 1)
        self.nc.vector.reciprocal(self.RV[:, :], self.RR[:, :]).then_inc(self.recip_done, 1)

    def prime(self, dve):
        dve.sem_inc(self.max_done, 2)
        dve.sem_inc(self.st_made, 1)
        dve.sem_inc(self.exp_done, 2)
        dve.sem_inc(self.pv_done, 4)
        dve.sem_inc(self.ctx_out, 2)
        dve.sem_inc(self.proj_out, 2)
        dve.sem_inc(self.ctx_in, 1)
        dve.sem_inc(self.post_done, 1)


class Chain:

    def __init__(self, sem, base=0):
        self.sem, self.base, self.n = sem, base, 0

    def did(self, ins):
        ins.then_inc(self.sem, 1)
        self.n += 1

    def wait(self, eng):
        eng.wait_ge(self.sem, self.base + self.n)


def layer0_attention(nc, g, x, cond, wq, wo, sel):
    c = Core(heads=8, n=T0, n_pre=4, n_post=4, mask_row=True, lag=4, dt=F32R)
    QSCALE = float((S0 // 8) ** -0.25)
    with ExitStack() as ctx:
        a = Attention(nc, ctx, "a0", c, g.ident)
        sb = lambda name, shape, dt: ctx.enter_context(nc.sbuf_tensor(f"a0_{name}", shape, dt))
        sem = lambda name: ctx.enter_context(nc.semaphore(f"a0_{name}"))
        xb = [sb(f"xb{i}", [P, 2, T0], F32) for i in range(2)]
        cb = [sb(f"cb{i}", [P, T0], F32) for i in range(2)]
        wn = sb("wn", [P, 2, 2, S0], F32)
        wT = sb("wT", [P, 2, 2, S0], F32)
        QM = sb("QM", [P, T0], F32)
        H = sb("H", [P, 2, T0], F32R)
        L = sb("L", [P, 2, T0], F32R)
        w_in, w_made, w_out = sem("w_in"), sem("w_made"), sem("w_out")
        x_in = [sem("x_in0"), sem("x_in1")]
        rows_done = sem("rows_done")
        rows_begun = sem("rows_begun")
        ones_set = sem("ones_set")

        with nc.Block() as block:
            def load(sp, n):
                if isinstance(n.idx, int) and n.idx < 2:
                    pass
                else:
                    sp.wait_ge(a.v_ready, n.idx - 1)
                    sp.wait_ge(rows_done, n.idx - 1)
                sp.dma_start(xb[n.par][:, :, :], x[n.idx].rearrange("(k p) t -> p k t", p=P)).then_inc(x_in[n.par], 16)
                sp.dma_start(cb[n.par][:, :], cond[bass.ds(n.idx, 1), :].to_broadcast([P, T0])).then_inc(x_in[n.par], 16)

            @block.sync
            def _(sp):
                for i, w in enumerate((wq, wo)):
                    sp.dma_start(wn[:, i, :, :], w.rearrange("(k p) d -> p k d", p=P)).then_inc(w_in, 16)
                sp.dma_start(a.SEL[:, :, :], sel).then_inc(w_in, 16)
                sp.dma_start(g.x1[:, :, :], x.rearrange("b (t p) f -> p (b t) f", p=P)).then_inc(g.x1_in, 16)
                b0, b1 = Batch(0, 0), Batch(0, 1)
                load(sp, b0)
                load(sp, b1)
                a.sp_assemble(sp, b0, H, L, H, L)
                a.sp_shift(sp, b0)

                def step(b, b1, b2):
                    if b1 is not None:
                        a.sp_assemble(sp, b1, H, L, H, L)
                    if b2 is not None:
                        load(sp, b2)
                    if b1 is not None:
                        a.sp_shift(sp, b1)
                    a.sp_context(sp, b)

                with sp.Fori(0, NB // 2 - 1) as i:
                    for q in range(2):
                        step(Batch(i, q), Batch(i, q + 1), Batch(i, q + 2))
                i = NB // 2 - 1
                step(Batch(i, 0), Batch(i, 1), None)
                step(Batch(i, 1), None, None)
                sp.wait_ge(g.x1_in, 16)

            @block.gpsimd
            def _(pool):
                pool.wait_ge(ones_set, 4)

                def rows(n):
                    pool.wait_ge(x_in[n.par], 32 * (n.half + 1))
                    if not n.first:
                        pool.wait_ge(a.st_made, c.slots * (n.idx - 1) + 1)
                    pool.sem_inc(rows_begun, 1)
                    src = cb[n.par][96:97, :].unsqueeze(1).to_broadcast([1, c.heads, T0])
                    nc.gpsimd.tensor_copy(a.A[n.par][96:97, :, :], src)
                    nc.gpsimd.tensor_scalar(a.B[n.par][96:97, :, :], src, -NEG, NEG, ALU.mult, ALU.add).then_inc(rows_done, 1)

                rows(Batch(0, 0))
                with pool.Fori(0, NB // 2 - 1) as i:
                    for q in range(2):
                        rows(Batch(i, q + 1))
                rows(Batch(NB // 2 - 1, 1))

            @block.tensor
            def _(pe):
                pe.wait_ge(w_in, 48)
                pe.wait_ge(g.ident_set, 2)
                for i in range(2):
                    for k in range(2):
                        for o in range(2):
                            mm = nc.tensor.transpose(a.pp[i][:, k * 256 + o * P:k * 256 + (o + 1) * P],
                                                     wn[:, i, o, k * P:(k + 1) * P], g.ident[:, :])
                    mm.then_inc(w_made, 1)
                pe.wait_ge(w_out, 2)

                def pre(n, uses):
                    pe.wait_ge(x_in[n.par], 32 * (n.half + 1))
                    for o in range(2):
                        bank = a.pe_take(pe, uses)
                        for k in range(2):
                            mm = nc.tensor.matmul(bank[:, :], wT[:, 0, k, o * P:(o + 1) * P], xb[n.par][:, k, :],
                                                  start=(k == 0), stop=(k == 1))
                        mm.then_inc(a.proj_made, 1)
                    for u in range(2):
                        bank = a.pe_take(pe, uses)
                        for t in range(2):
                            for k in range(2):
                                mm = nc.tensor.matmul(bank[:, t * S0:(t + 1) * S0],
                                                      xb[n.par][:, k, (2 * u + t) * P:(2 * u + t + 1) * P],
                                                      wT[:, 0, k, :], start=(k == 0), stop=(k == 1))
                        mm.then_inc(a.proj_made, 1)

                def post(n, uses):
                    a.pe_spread(pe, n, uses)
                    pe.wait_ge(a.ctx_norm, 2 * (n.idx + 1))
                    for u in range(2):
                        bank = a.pe_take(pe, uses)
                        for t in range(2):
                            for k in range(2):
                                mm = nc.tensor.matmul(bank[:, t * S0:(t + 1) * S0],
                                                      a.CN[:, k, (2 * u + t) * P:(2 * u + t + 1) * P],
                                                      wT[:, 1, k, :], start=(k == 0), stop=(k == 1))
                        mm.then_inc(a.proj_made, 1)

                b0 = Batch(0, 0)
                uses = Uses(0, 0)
                pre(b0, uses)
                pe.wait_ge(rows_done, 1)
                for s in range(c.slots):
                    a.pe_nat(pe, b0, s)
                a.pe_shift(pe, b0, uses)
                pre(Batch(0, 1), uses)

                def step(b, b1, b2, uses):
                    if b1 is not None:
                        pe.wait_ge(rows_done, b1.idx + 1)
                    a.pe_slots(pe, b, b1)
                    if b1 is not None:
                        a.pe_shift(pe, b1, uses)
                    if b2 is not None:
                        pre(b2, uses)
                    post(b, uses)

                with pe.Fori(0, NB // 2 - 1) as i:
                    for q in range(2):
                        b = Batch(i, q)
                        step(b, Batch(i, q + 1), Batch(i, q + 2), c.uses_at(b, q))
                i = NB // 2 - 1
                uses = c.uses_at(Batch(i, 0), 0)
                step(Batch(i, 0), Batch(i, 1), None, uses)
                step(Batch(i, 1), None, None, uses)

            @block.scalar
            def _(act):
                with act.Fori(0, NB // 2) as i:
                    for q in range(2):
                        a.act_slots(act, Batch(i, q))

            @block.vector
            def _(dve):
                a.prime(dve)
                for i in range(2):
                    nc.vector.memset(a.B[i][96:98, :, :].bitcast(F32), 1.0).then_inc(ones_set, 1)
                for i in range(2):
                    nc.vector.memset(a.V[i][:, :, :, :], 1.0).then_inc(ones_set, 1)
                dve.wait_ge(ones_set, 4)
                for i in range(2):
                    dve.wait_ge(w_made, i + 1)
                    nc.vector.tensor_copy(wT[:, i, :, :], a.pp[i][:, :].rearrange("p (k o) -> p k o", k=2)).then_inc(w_out, 1)

                steps = a.dve_step

                def pre(n, uses, chain):
                    for o in range(2):
                        bank = a.dve_wait(dve, uses)
                        dve.wait_ge(x_in[n.par], 32 * (n.half + 1))
                        if o == 0 and not n.first:
                            dve.wait_ge(a.ab_in, 16 * a.AB_DMAS * n.idx)
                        chain.wait(dve)
                        chain.did(nc.vector.scalar_tensor_tensor(out=QM[:, :], in0=bank[:, :], scalar=QSCALE,
                                                                 in1=cb[n.par][:, :], op0=ALU.mult, op1=ALU.mult))
                        chain.wait(dve)
                        dve.sem_inc(a.proj_out, 1)
                        chain.did(nc.vector.tensor_copy(H[:, o, :], QM[:, :]))
                        chain.wait(dve)
                        chain.did(nc.vector.tensor_tensor(L[:, o, :], QM[:, :], H[:, o, :].bitcast(F32), ALU.subtract))
                    chain.wait(dve)
                    dve.sem_inc(a.split_done, 1)
                    for u in range(2):
                        bank = a.dve_wait(dve, uses)
                        nc.vector.tensor_copy(a.V[n.par][:, 2 * u:2 * u + 2, :, 0:32],
                                              bank[:, :].rearrange("p (t h d) -> p t h d", t=2, h=c.heads)).then_inc(a.proj_out, 1)
                    dve.wait_ge(a.proj_out, uses.base + uses.k + 2)
                    dve.sem_inc(a.v_ready, 1)

                def post(n, uses, chain):
                    a.dve_recip(dve, n)
                    for u in range(2):
                        bank = a.dve_wait(dve, uses)
                        nc.vector.tensor_tensor(a.CN[:, u, :], a.CT[:, u, :], bank[:, :], ALU.mult).then_inc(a.ctx_norm, 1)
                        dve.wait_ge(a.ctx_norm, 2 * n.idx + u + 1)
                        dve.sem_inc(a.proj_out, 1)
                    dve.sem_inc(a.post_done, 1)
                    for u in range(2):
                        bank = a.dve_wait(dve, uses)
                        ps = bank[:, :].rearrange("p (t s) -> p t s", t=2)
                        hi = g.XTh[:, 2 * u:2 * u + 2, bass.ds(n.idx * S0, S0)]
                        lo = g.XTl[:, 2 * u:2 * u + 2, bass.ds(n.idx * S0, S0)]
                        chain.did(nc.vector.tensor_copy(hi, ps))
                        chain.wait(dve)
                        nc.vector.tensor_tensor(lo, ps, hi, ALU.subtract).then_inc(a.proj_out, 1)

                PRE_STEPS, POST_STEPS = 6, 2
                per = PRE_STEPS + POST_STEPS
                b0 = Batch(0, 0)
                uses, chain = Uses(0, 0), Chain(steps, 0)
                pre(b0, uses, chain)
                for s in range(c.slots):
                    a.dve_max(dve, b0, s)
                a.dve_shift(dve, b0, uses)
                pre(Batch(0, 1), uses, chain)

                def step(b, b1, b2, uses, chain):
                    if b1 is not None:
                        for s in range(c.slots):
                            a.dve_max(dve, b1, s)
                        a.dve_shift(dve, b1, uses)
                    if b2 is not None:
                        pre(b2, uses, chain)
                    post(b, uses, chain)

                with dve.Fori(0, NB // 2 - 1) as i:
                    for q in range(2):
                        b = Batch(i, q)
                        step(b, Batch(i, q + 1), Batch(i, q + 2), c.uses_at(b, q), Chain(steps, 2 * PRE_STEPS + per * b.idx))
                i = NB // 2 - 1
                b = Batch(i, 0)
                uses, chain = c.uses_at(b, 0), Chain(steps, 2 * PRE_STEPS + per * b.idx)
                step(b, Batch(i, 1), None, uses, chain)
                step(Batch(i, 1), None, None, uses, chain)


def route_vector(nc, dve, r, logits, chain):
    V = nc.vector
    over = lambda ap: ap.unsqueeze(2).to_broadcast([P, NT, E])

    def did(ins):
        chain.did(ins)
        chain.wait(dve)

    def pick(l, m, oh):
        did(V.tensor_reduce(m, l, AX, ALU.max))
        did(V.tensor_tensor(r.t[:, :, :], l, over(m), ALU.is_equal))
        did(V.tensor_tensor(r.t[:, :, :], r.t[:, :, :], r.desc[:, :, :], ALU.mult))
        did(V.tensor_reduce(r.k[:, :], r.t[:, :, :], AX, ALU.max))
        did(V.tensor_tensor(oh, r.desc[:, :, :], over(r.k[:, :]), ALU.is_equal))

    did(V.tensor_scalar(r.l[:, :, :], logits, 1.0 / WS, None, ALU.mult))
    pick(r.l[:, :, :], r.m1[:, :], r.oh1[:, :, :])
    did(V.scalar_tensor_tensor(out=r.l2[:, :, :], in0=r.oh1[:, :, :], scalar=-BIG, in1=r.l[:, :, :],
                               op0=ALU.mult, op1=ALU.add))
    pick(r.l2[:, :, :], r.m2[:, :], r.oh2[:, :, :])


class Router:
    def __init__(self, nc, ctx, tag):
        sb = lambda name, shape: ctx.enter_context(nc.sbuf_tensor(f"{tag}_{name}", shape, F32))
        self.l, self.l2, self.t, self.oh1, self.oh2, self.desc, self.ex = (
            sb(n, [P, NT, E]) for n in ("l", "l2", "t", "oh1", "oh2", "desc", "ex"))
        self.k, self.m1, self.m2, self.w1, self.w2, self.s = (
            sb(n, [P, NT]) for n in ("k", "m1", "m2", "w1", "w2", "s"))


def layer0_experts(nc, g, w_router, w_gate, w_up, w_down, desc):
    CH = 512
    NC = NB * S0 // CH
    with ExitStack() as ctx:
        sb = lambda name, shape, dt: ctx.enter_context(nc.sbuf_tensor(f"b_{name}", shape, dt))
        sem = lambda name: ctx.enter_context(nc.semaphore(f"b_{name}"))
        ps = lambda name: ctx.enter_context(nc.psum_tensor(f"b_{name}", [P, 512], F32))
        r = Router(nc, ctx, "b")
        coef = sb("coef", [P, NT, E], F32)
        wrs = sb("wrs", [P, KF, E], F32)
        wrh = sb("wrh", [P, KF, E], F16)
        wrl = sb("wrl", [P, KF, E], F16)
        stage = sb("stage", [P, 2 * KF * F0 + 3 * T0], F32)
        GU = KF * F0
        wh = [sb(f"wh{i}", [P, 2 * GU + 3 * T0], F16) for i in range(2)]
        wl = [sb(f"wl{i}", [P, 2 * GU + 3 * T0], F16) for i in range(2)]
        SG = [sb(f"SG{i}", [P, CH], F32) for i in range(2)]
        HF = sb("HF", [P, CH], F32)
        HH = sb("HH", [P, 3, CH], F16)
        HL = sb("HL", [P, 3, CH], F16)
        G = [ps(f"G{i}") for i in range(2)]
        U = [ps(f"U{i}") for i in range(2)]
        O = [ps(f"O{i}") for i in range(4)]
        r_in, st_in = sem("r_in"), sem("st_in")
        st_clear = sem("st_clear")
        w_hi, w_lo = sem("w_hi"), sem("w_lo")
        wr_hi, wr_lo = sem("wr_hi"), sem("wr_lo")
        logits, routed, ex_done = sem("logits"), sem("routed"), sem("ex_done")
        made, silu, mult = sem("made"), sem("silu"), sem("mult")
        hid, down, added = sem("hid"), sem("down"), sem("added")
        step_sem, gate = sem("dve_step"), sem("gate")

        def part(w, which):
            if which < 2:
                return w[:, which * GU:(which + 1) * GU].rearrange("p (k f) -> p k f", k=KF)
            return w[:, 2 * GU:].rearrange("p (k f) -> p k f", k=3)

        def tile_no(e, cc):
            return NC * e + cc

        with nc.Block() as block:
            @block.sync
            def _(sp):
                sp.dma_start(wrs[:, :, :], w_router.rearrange("(k p) e -> p k e", p=P)).then_inc(r_in, 16)
                sp.dma_start(r.desc[:, :, :], desc).then_inc(r_in, 16)
                sp.wait_ge(st_clear, 1)

                def load(e):
                    sp.dma_start(part(stage, 0), w_gate[e].rearrange("(k p) f -> p k f", p=P)).then_inc(st_in, 16)
                    sp.dma_start(part(stage, 1), w_up[e].rearrange("(k p) f -> p k f", p=P)).then_inc(st_in, 16)
                    d = part(stage, 2)
                    sp.dma_start(d[:, 0:2, :], w_down[e][0:2 * P, :].rearrange("(k p) f -> p k f", p=P)).then_inc(st_in, 16)
                    sp.dma_start(d[0:F0 - 2 * P, 2, :], w_down[e][2 * P:F0, :]).then_inc(st_in, 16)

                load(0)
                with sp.Fori(1, E) as e:
                    sp.wait_ge(w_lo, e)
                    load(e)

            @block.tensor
            def _(pe):
                pe.wait_ge(wr_lo, 1)
                for t in range(NT):
                    n = 0
                    for k in range(KF):
                        for xs, ws in ((g.XTh, wrh), (g.XTl, wrh), (g.XTh, wrl)):
                            mm = nc.tensor.matmul(O[0][:, t * E:(t + 1) * E], xs[:, k, t * P:(t + 1) * P], ws[:, k, :],
                                                  start=(n == 0), stop=(n == 3 * KF - 1))
                            n += 1
                mm.then_inc(logits, 1)

                def step(e, q, cc, rr):
                    s = tile_no(e, cc)
                    if rr == 0:
                        pe.wait_ge(w_lo, e + 1)
                    toks = bass.ds(cc * CH, CH)
                    for ft, (f0, m) in enumerate(F0_TILES):
                        j = (rr + ft) % 2
                        pe.wait_ge(mult, 3 * s + ft + 1)
                        for which, bank in ((0, G[j]), (1, U[j])):
                            h, l = part(wh[q], which), part(wl[q], which)
                            n = 0
                            for k in range(KF):
                                for w, xs in ((h, g.XTh), (h, g.XTl), (l, g.XTh)):
                                    mm = nc.tensor.matmul(bank[0:m, :], w[:, k, f0:f0 + m], xs[:, k, toks],
                                                          start=(n == 0), stop=(n == 3 * KF - 1))
                                    n += 1
                        mm.then_inc(made, 1)
                    dh, dl = part(wh[q], 2), part(wl[q], 2)
                    for k, (f0, m) in enumerate(F0_TILES):
                        pe.wait_ge(hid, 3 * s + k + 2)
                        for t in range(4):
                            if k == 0:
                                pe.wait_ge(added, 4 * s + t + 1)
                            for n, (hs, ws) in enumerate(((HH, dh), (HH, dl), (HL, dh))):
                                mm = nc.tensor.matmul(O[t][:, :], hs[0:m, k, t * P:(t + 1) * P], ws[0:m, k, :],
                                                      start=(k == 0 and n == 0), stop=(k == 2 and n == 2))
                            if k == 2:
                                mm.then_inc(down, 1)

                pe.wait_ge(routed, 1)
                with pe.Fori(0, E // 2) as ep:
                    for q in range(2):
                        with pe.Fori(0, NC // 2) as cp:
                            for rr in range(2):
                                step(2 * ep + q, q, 2 * cp + rr, rr)

            def experts(eng, split_one, step):
                def expert(e, q, last):
                    if not last:
                        split_one(e + 1, 1 - q)
                    with eng.Fori(0, NC // 2) as cp:
                        for rr in range(2):
                            step(e, 2 * cp + rr, rr)
                split_one(0, 0)
                with eng.Fori(0, E // 2 - 1) as ep:
                    for q in range(2):
                        expert(2 * ep + q, q, False)
                expert(E - 2, 0, False)
                expert(E - 1, 1, True)

            @block.scalar
            def _(act):
                act.wait_ge(r_in, 32)
                nc.scalar.activation(wrh[:, :, :], wrs[:, :, :], ACT.Copy, scale=WS).then_inc(wr_hi, 1)

                def split_one(e, q):
                    act.wait_ge(st_in, 64 * (e + 1))
                    act.wait_ge(down, 4 * tile_no(e - 1, 0) + 4 if not isinstance(e, int) or e else 4)
                    nc.scalar.activation(wh[q][:, :], stage[:, :], ACT.Copy, scale=WS).then_inc(w_hi, 1)

                def step(e, cc, rr):
                    s = tile_no(e, cc)
                    for ft, (f0, m) in enumerate(F0_TILES):
                        j = (rr + ft) % 2
                        act.wait_ge(mult, 3 * s + ft + 1)
                        act.wait_ge(made, 3 * s + ft + 1)
                        nc.scalar.activation(SG[j][0:m, :], G[j][0:m, :], ACT.Silu, scale=1.0 / WS).then_inc(silu, 1)

                act.wait_ge(routed, 1)
                nc.scalar.activation(r.w2[:, :], r.s[:, :], ACT.Exp).then_inc(ex_done, 1)
                experts(act, split_one, step)

            @block.vector
            def _(dve):
                chain = Chain(step_sem)

                def did(ins):
                    chain.did(ins)
                    chain.wait(dve)

                V = nc.vector
                V.memset(stage[:, :], 0.0).then_inc(st_clear, 1)
                dve.sem_inc(mult, 2)
                dve.sem_inc(hid, 1)
                dve.sem_inc(down, 4)
                dve.sem_inc(added, 4)
                dve.wait_ge(wr_hi, 1)
                V.scalar_tensor_tensor(out=wrl[:, :, :], in0=wrs[:, :, :], scalar=WS, in1=wrh[:, :, :],
                                       op0=ALU.mult, op1=ALU.subtract).then_inc(wr_lo, 1)
                dve.wait_ge(logits, 1)
                route_vector(nc, dve, r, O[0][:, 0:NT * E].rearrange("p (t e) -> p t e", t=NT), chain)
                did(V.tensor_tensor(r.s[:, :], r.m2[:, :], r.m1[:, :], ALU.subtract))
                dve.sem_inc(routed, 1)
                dve.wait_ge(ex_done, 1)
                did(V.tensor_scalar(r.w1[:, :], r.w2[:, :], 1.0, None, ALU.add))
                did(V.reciprocal(r.w1[:, :], r.w1[:, :]))
                did(V.tensor_tensor(r.w2[:, :], r.w2[:, :], r.w1[:, :], ALU.mult))
                over = lambda ap: ap.unsqueeze(2).to_broadcast([P, NT, E])
                did(V.tensor_tensor(r.t[:, :, :], r.oh1[:, :, :], over(r.w1[:, :]), ALU.mult))
                did(V.tensor_tensor(r.l2[:, :, :], r.oh2[:, :, :], over(r.w2[:, :]), ALU.mult))
                did(V.tensor_tensor(r.t[:, :, :], r.t[:, :, :], r.l2[:, :, :], ALU.add))
                did(V.tensor_scalar(coef[:, :, :], r.t[:, :, :], 1.0 / WS, None, ALU.mult))

                def split_one(e, q):
                    dve.wait_ge(w_hi, e + 1)
                    V.scalar_tensor_tensor(out=wl[q][:, :], in0=stage[:, :], scalar=WS, in1=wh[q][:, :],
                                           op0=ALU.mult, op1=ALU.subtract).then_inc(w_lo, 1)

                base = chain.n

                def step(e, cc, rr):
                    s = tile_no(e, cc)
                    for ft, (f0, m) in enumerate(F0_TILES):
                        j, i = (rr + ft) % 2, 3 * s + ft
                        dve.wait_ge(silu, i + 1)
                        dve.wait_ge(hid, i + 1)
                        V.scalar_tensor_tensor(out=HF[0:m, :], in0=U[j][0:m, :], scalar=1.0 / WS, in1=SG[j][0:m, :],
                                               op0=ALU.mult, op1=ALU.mult).then_inc(mult, 1)
                        dve.wait_ge(mult, i + 3)
                        dve.wait_ge(down, 4 * s + 4)
                        V.tensor_copy(HH[0:m, ft, :], HF[0:m, :]).then_inc(step_sem, 1)
                        dve.wait_ge(step_sem, base + i + 1)
                        V.tensor_tensor(HL[0:m, ft, :], HF[0:m, :], HH[0:m, ft, :], ALU.subtract).then_inc(hid, 1)
                    for t in range(4):
                        dve.wait_ge(down, 4 * s + t + 5)
                        acc = g.x1[:, 4 * cc + t, :]
                        V.scalar_tensor_tensor(out=acc, in0=O[t][:, :], scalar=coef[:, 4 * cc + t, bass.ds(e, 1)],
                                               in1=acc, op0=ALU.mult, op1=ALU.add).then_inc(added, 1)

                experts(dve, split_one, step)


def layer1_attention(nc, g, cond, w_emb, b_emb, g_norm, w_qkv, g_q, g_k, w_out, sel):
    c = Core(heads=16, n=S0, n_pre=12, n_post=4, mask_row=False, lag=6, dt=F16)
    EPS = 1e-6
    D = T0 // c.heads
    with ExitStack() as ctx:
        a = Attention(nc, ctx, "c", c, g.ident)
        sb = lambda name, shape, dt: ctx.enter_context(nc.sbuf_tensor(f"c_{name}", shape, dt))
        sem = lambda name: ctx.enter_context(nc.semaphore(f"c_{name}"))
        wqh = sb("wqh", [P, KF, 3 * T0], F16)
        wql = sb("wql", [P, KF, 3 * T0], F16)
        woh = sb("woh", [P, KF, T0], F16)
        wol = sb("wol", [P, KF, T0], F16)
        gcol = sb("gcol", [P, 2], F32)
        gs = sb("gs", [P, KF, NB], F32)
        sh = sb("sh", [P, KF, NB], F32)
        rstd = sb("rstd", [P, NT], F32)
        XX = sb("XX", [P, 4 * T0], F32)
        XS = XX[:, 0:2 * T0].rearrange("p (t f) -> p t f", t=2)
        XN = XX[:, 2 * T0:4 * T0].rearrange("p (k s) -> p k s", k=KF)
        SQ = XX[:, :].rearrange("p (t w f) -> p t w f", t=2, w=2)
        XNh = sb("XNh", [P, KF, S0], F16)
        XNl = sb("XNl", [P, KF, S0], F16)
        QK = sb("QK", [P, 2, 2, T0], F32)
        ssq = sb("ssq", [P, 2 * 2 * 16], F32)
        H = [sb(f"H{i}", [P, KF, S0], F16) for i in range(2)]
        L = [sb(f"L{i}", [P, KF, S0], F16) for i in range(2)]
        CH = sb("CH", [P, KF, S0], F16)
        CL = sb("CL", [P, KF, S0], F16)
        p_in, q_in, p_act, p_dve, p_pe = sem("p_in"), sem("q_in"), sem("p_act"), sem("p_dve"), sem("p_pe")
        p_sq = sem("p_sq")
        xs_done, xn_done, qk_out, sq_done, var_done, std_done, qn_done = (
            sem(n) for n in ("xs_done", "xn_done", "qk_out", "sq_done", "var_done", "std_done", "qn_done"))

        with ExitStack() as setup:
            tmp = lambda name, shape: setup.enter_context(nc.sbuf_tensor(f"cs_{name}", shape, F32))
            ws = QK[:, :, :, :].rearrange("p a b f -> p (a b) f")
            cn = a.CS[0:NB, 0:2, :].rearrange("b a f -> b (a f)")
            condT = tmp("condT", [P, KF, NB])
            vrow = a.CS[0:3 * KF, 2, 0:P]
            vec = tmp("vec", [P, 3, KF])
            with nc.Block() as block:
                @block.sync
                def _(sp):
                    sp.dma_start(cn, cond).then_inc(p_in, 16)
                    sp.dma_start(vrow[0:2 * KF, :], b_emb.rearrange("(k p) -> k p", p=P)).then_inc(p_in, 16)
                    sp.dma_start(vrow[2 * KF:3 * KF, :], g_norm.rearrange("(k p) -> k p", p=P)).then_inc(p_in, 16)
                    for j in range(4):
                        for i, v in enumerate((g_q, g_k)):
                            sp.dma_start(gcol[32 * j:32 * j + 32, i:i + 1], v.rearrange("(p a) -> p a", a=1)).then_inc(p_in, 16)
                    sp.dma_start(a.SEL[:, :, :], sel).then_inc(p_in, 16)
                    for i in range(6):
                        src = (w_qkv[:, i * T0:(i + 1) * T0] if i < 3 else w_out if i == 3
                               else w_emb[:, (i - 4) * T0:(i - 3) * T0])
                        if i:
                            sp.wait_ge(p_dve, i) if i < 5 else sp.wait_ge(p_pe, 2)
                        sp.dma_start(ws[:, :, :], src.rearrange("(k p) f -> p k f", p=P)).then_inc(q_in, 16)

                @block.scalar
                def _(act):
                    for i in range(4):
                        act.wait_ge(q_in, 16 * (i + 1))
                        dst = wqh[:, :, i * T0:(i + 1) * T0] if i < 3 else woh[:, :, :]
                        nc.scalar.activation(dst, ws[:, :, :], ACT.Copy, scale=WS).then_inc(p_act, 1)
                    for t in range(NT):
                        if t >= 4:
                            act.wait_ge(p_sq, t - 3)
                        nc.scalar.activation(XX[:, t % 4 * T0:(t % 4 + 1) * T0], g.x1[:, t, :], ACT.Square,
                                             accum_out=rstd[:, t:t + 1]).then_inc(p_sq, 1)
                    act.wait_ge(p_dve, 11)
                    nc.scalar.activation(rstd[:, :], rstd[:, :], ACT.Sqrt).then_inc(p_act, 1)

                @block.tensor
                def _(pe):
                    pe.wait_ge(p_in, 16 * 12)
                    for k in range(KF):
                        mm = nc.tensor.transpose(a.pp[0][:, k * NB:(k + 1) * NB], cn[:, k * P:(k + 1) * P], g.ident[0:NB, 0:NB])
                    mm = nc.tensor.transpose(a.pp[0][:, KF * NB:KF * NB + 3 * KF], vrow, g.ident[0:3 * KF, 0:3 * KF])
                    mm.then_inc(p_pe, 1)
                    pe.wait_ge(p_dve, 5)
                    for i in range(2):
                        pe.wait_ge(q_in, 16 * (5 + i))
                        for o in range(KF):
                            for k in range(KF):
                                mm = nc.tensor.matmul(a.pp[1][:, (i * KF + o) * NB:(i * KF + o + 1) * NB],
                                                      ws[:, k, o * P:(o + 1) * P], condT[:, k, :],
                                                      start=(k == 0), stop=(k == KF - 1))
                        mm.then_inc(p_pe, 1)

                @block.vector
                def _(dve):
                    V = nc.vector
                    for i in range(4):
                        dve.wait_ge(p_act, i + 1)
                        hi, dst = ((wqh[:, :, i * T0:(i + 1) * T0], wql[:, :, i * T0:(i + 1) * T0]) if i < 3
                                   else (woh[:, :, :], wol[:, :, :]))
                        V.scalar_tensor_tensor(out=dst, in0=ws[:, :, :], scalar=WS, in1=hi,
                                               op0=ALU.mult, op1=ALU.subtract).then_inc(p_dve, 1)
                    dve.wait_ge(p_pe, 1)
                    V.tensor_copy(condT[:, :, :], a.pp[0][:, 0:KF * NB].rearrange("p (k b) -> p k b", k=KF)).then_inc(p_dve, 1)
                    V.tensor_copy(vec[:, :, :], a.pp[0][:, KF * NB:KF * NB + 3 * KF].rearrange("p (s k) -> p s k", s=3)).then_inc(p_dve, 1)
                    dve.wait_ge(p_dve, 6)
                    dve.wait_ge(p_pe, 3)
                    ss = a.pp[1][:, 0:2 * KF * NB].rearrange("p (s k b) -> p s k b", s=2, k=KF)
                    over = lambda ap: ap.unsqueeze(2).to_broadcast([P, KF, NB])
                    V.tensor_tensor(sh[:, :, :], ss[:, 1, :, :], over(vec[:, 1, :]), ALU.add).then_inc(p_dve, 1)
                    V.tensor_tensor(gs[:, :, :], ss[:, 0, :, :], over(vec[:, 0, :]), ALU.add).then_inc(p_dve, 1)
                    dve.wait_ge(p_dve, 8)
                    V.scalar_tensor_tensor(out=gs[:, :, :], in0=gs[:, :, :], scalar=1.0, in1=over(vec[:, 2, :]),
                                           op0=ALU.add, op1=ALU.mult).then_inc(p_dve, 1)
                    dve.wait_ge(p_sq, NT)
                    V.tensor_scalar(rstd[:, :], rstd[:, :], 1.0 / T0, EPS, ALU.mult, ALU.add).then_inc(p_dve, 1)
                    dve.wait_ge(p_dve, 10)
                    V.reciprocal(rstd[:, :], rstd[:, :]).then_inc(p_dve, 1)
                    V.tensor_scalar(gcol[:, 0:1], gcol[:, 0:1], float(D ** -0.5), None, ALU.mult).then_inc(p_dve, 1)
                    dve.wait_ge(p_dve, 12)
                    for i in range(2):
                        V.memset(a.B[i][96:97, :, :], 1.0).then_inc(p_dve, 1)
                        V.memset(a.V[i][:, :, :, :], 1.0).then_inc(p_dve, 1)

        with nc.Block() as block:
            @block.sync
            def _(sp):
                b0 = Batch(0, 0)
                a.sp_assemble(sp, b0, H[0], L[0], H[1], L[1])
                a.sp_shift(sp, b0)

                def step(b, b1):
                    if b1 is not None:
                        a.sp_assemble(sp, b1, H[0], L[0], H[1], L[1])
                        a.sp_shift(sp, b1)
                    a.sp_context(sp, b)

                with sp.Fori(0, NB // 2 - 1) as i:
                    for q in range(2):
                        step(Batch(i, q), Batch(i, q + 1))
                i = NB // 2 - 1
                step(Batch(i, 0), Batch(i, 1))
                step(Batch(i, 1), None)

            @block.tensor
            def _(pe):
                def pre_qkv(n, uses):
                    pe.wait_ge(xs_done, n.idx + 1)
                    for u in range(2):
                        bank = a.pe_take(pe, uses)
                        for kk in range(2):
                            for t in range(2):
                                mm = nc.tensor.transpose(bank[:, kk * S0 + t * P:kk * S0 + (t + 1) * P],
                                                         XS[:, t, (2 * u + kk) * P:(2 * u + kk + 1) * P], g.ident[:, :])
                        mm.then_inc(a.proj_made, 1)
                    pe.wait_ge(xn_done, 2 * (n.idx + 1))
                    for t in range(2):
                        for j in range(3):
                            bank = a.pe_take(pe, uses)
                            for k in range(KF):
                                for m, (xs, ws) in enumerate(((XNh, wqh), (XNh, wql), (XNl, wqh))):
                                    mm = nc.tensor.matmul(bank[:, :], xs[:, k, t * P:(t + 1) * P],
                                                          ws[:, k, j * T0:(j + 1) * T0],
                                                          start=(k == 0 and m == 0), stop=(k == KF - 1 and m == 2))
                            mm.then_inc(a.proj_made, 1)

                def pre_qk(n, uses):
                    pe.wait_ge(qn_done, n.idx + 1)
                    for w in range(2):
                        for u in range(2):
                            bank = a.pe_take(pe, uses)
                            for kk in range(2):
                                for t in range(2):
                                    mm = nc.tensor.transpose(bank[:, kk * S0 + t * P:kk * S0 + (t + 1) * P],
                                                             QK[:, t, w, (2 * u + kk) * P:(2 * u + kk + 1) * P], g.ident[:, :])
                            mm.then_inc(a.proj_made, 1)

                def post(n, uses):
                    a.pe_spread(pe, n, uses)
                    pe.wait_ge(a.ctx_norm, 2 * (n.idx + 1))
                    for u in range(2):
                        bank = a.pe_take(pe, uses)
                        for dd in range(2):
                            d = 2 * u + dd
                            for k in range(KF):
                                for m, (ws, xs) in enumerate(((woh, CH), (woh, CL), (wol, CH))):
                                    mm = nc.tensor.matmul(bank[:, dd * S0:(dd + 1) * S0], ws[:, k, d * P:(d + 1) * P],
                                                          xs[:, k, :], start=(k == 0 and m == 0),
                                                          stop=(k == KF - 1 and m == 2))
                        mm.then_inc(a.proj_made, 1)

                b0, b1 = Batch(0, 0), Batch(0, 1)
                uses = Uses(0, 0)
                pre_qkv(b0, uses)
                pre_qk(b0, uses)
                for s in range(c.slots):
                    a.pe_nat(pe, b0, s)
                a.pe_shift(pe, b0, uses)
                pre_qkv(b1, uses)
                pre_qk(b1, uses)

                def step(b, b1, b2, uses):
                    a.pe_slots(pe, b, b1)
                    if b1 is not None:
                        a.pe_shift(pe, b1, uses)
                    if b2 is not None:
                        pre_qkv(b2, uses)
                    post(b, uses)
                    if b2 is not None:
                        pre_qk(b2, uses)

                with pe.Fori(0, NB // 2 - 1) as i:
                    for q in range(2):
                        b = Batch(i, q)
                        step(b, Batch(i, q + 1), Batch(i, q + 2), c.uses_at(b, q))
                i = NB // 2 - 1
                uses = c.uses_at(Batch(i, 0), 0)
                step(Batch(i, 0), Batch(i, 1), None, uses)
                step(Batch(i, 1), None, None, uses)

            @block.scalar
            def _(act):
                def stats(n):
                    act.wait_ge(qk_out, 4 * (n.idx + 1))
                    nc.scalar.activation(SQ[:, :, :, :], QK[:, :, :, :], ACT.Square).then_inc(sq_done, 1)
                    act.wait_ge(var_done, n.idx + 1)
                    nc.scalar.activation(ssq[:, :], ssq[:, :], ACT.Sqrt).then_inc(std_done, 1)

                stats(Batch(0, 0))
                stats(Batch(0, 1))
                with act.Fori(0, NB // 2 - 1) as i:
                    for q in range(2):
                        a.act_slots(act, Batch(i, q))
                        stats(Batch(i, q + 2))
                a.act_slots(act, Batch(NB // 2 - 1, 0))
                a.act_slots(act, Batch(NB // 2 - 1, 1))

            @block.vector
            def _(dve):
                V = nc.vector
                a.prime(dve)

                def pre_qkv(n, uses, chain):
                    for t in range(2):
                        ins = V.tensor_scalar(XS[:, t, :], g.x1[:, 2 * n.idx + t, :],
                                              rstd[:, bass.ds(2 * n.idx + t, 1)], None, ALU.mult)
                        if t == 0:
                            chain.did(ins)
                    chain.wait(dve)
                    ins.then_inc(xs_done, 1)
                    for u in range(2):
                        bank = a.dve_wait(dve, uses)
                        for kk in range(2):
                            k = 2 * u + kk
                            ins = V.tensor_scalar(XN[:, k, :], bank[:, kk * S0:(kk + 1) * S0], gs[:, k, bass.ds(n.idx, 1)],
                                                  sh[:, k, bass.ds(n.idx, 1)], ALU.mult, ALU.add)
                            chain.did(ins)
                        chain.wait(dve)
                        dve.sem_inc(a.proj_out, 1)
                        ks = slice(2 * u, 2 * u + 2)
                        chain.did(V.tensor_copy(XNh[:, ks, :], XN[:, ks, :]))
                        chain.wait(dve)
                        V.tensor_tensor(XNl[:, ks, :], XN[:, ks, :], XNh[:, ks, :], ALU.subtract).then_inc(xn_done, 1)
                    for t in range(2):
                        for w in range(2):
                            bank = a.dve_wait(dve, uses)
                            V.tensor_scalar(QK[:, t, w, :], bank[:, :], 1.0 / WS, None, ALU.mult).then_inc(qk_out, 1)
                            dve.wait_ge(qk_out, 4 * n.idx + 2 * t + w + 1)
                            dve.sem_inc(a.proj_out, 1)
                        bank = a.dve_wait(dve, uses)
                        V.tensor_scalar(a.V[n.par][:, t, :, 0:32], bank[:, :].rearrange("p (h d) -> p h d", h=c.heads),
                                        1.0 / WS, None, ALU.mult).then_inc(a.proj_out, 1)
                    dve.wait_ge(a.proj_out, uses.base + uses.k + 2)
                    dve.sem_inc(a.v_ready, 1)

                def pre_norm(n, uses, chain):
                    heads = lambda ap: ap.rearrange("p t w (h d) -> p (t w h) d", d=D)
                    dve.wait_ge(sq_done, n.idx + 1)
                    chain.did(V.tensor_reduce(ssq[:, :], heads(SQ[:, :, :, :]), AX, ALU.add))
                    chain.wait(dve)
                    chain.did(V.tensor_scalar(ssq[:, :], ssq[:, :], 1.0 / D, EPS, ALU.mult, ALU.add))
                    chain.wait(dve)
                    V.reciprocal(ssq[:, :], ssq[:, :]).then_inc(var_done, 1)
                    dve.wait_ge(std_done, n.idx + 1)
                    qk = heads(QK[:, :, :, :])
                    V.tensor_tensor(qk, qk, ssq[:, :].unsqueeze(2).to_broadcast([P, 64, D]), ALU.mult).then_inc(qn_done, 1)

                def pre_qk(n, uses, chain):
                    for w in range(2):
                        for u in range(2):
                            bank = a.dve_wait(dve, uses)
                            if w == 0 and u == 0 and not n.first:
                                dve.wait_ge(a.ab_in, 16 * a.AB_DMAS * n.idx)
                            ks = slice(2 * u, 2 * u + 2)
                            ps = bank[:, :].rearrange("p (k s) -> p k s", k=2)
                            chain.did(V.tensor_scalar(H[w][:, ks, :], ps, gcol[:, w:w + 1], None, ALU.mult))
                            chain.wait(dve)
                            chain.did(V.scalar_tensor_tensor(out=L[w][:, ks, :], in0=ps, scalar=gcol[:, w:w + 1],
                                                             in1=H[w][:, ks, :], op0=ALU.mult, op1=ALU.subtract))
                            chain.wait(dve)
                            dve.sem_inc(a.proj_out, 1)
                    dve.sem_inc(a.split_done, 1)

                def post(n, uses, chain):
                    a.dve_recip(dve, n)
                    for u in range(2):
                        bank = a.dve_wait(dve, uses)
                        ks = slice(2 * u, 2 * u + 2)
                        chain.did(V.tensor_tensor(a.CN[:, ks, :], a.CT[:, ks, :],
                                                  bank[:, :].rearrange("p (k s) -> p k s", k=2), ALU.mult))
                        chain.wait(dve)
                        dve.sem_inc(a.proj_out, 1)
                        chain.did(V.tensor_copy(CH[:, ks, :], a.CN[:, ks, :]))
                        chain.wait(dve)
                        V.tensor_tensor(CL[:, ks, :], a.CN[:, ks, :], CH[:, ks, :], ALU.subtract).then_inc(a.ctx_norm, 1)
                    dve.sem_inc(a.post_done, 1)
                    for u in range(2):
                        bank = a.dve_wait(dve, uses)
                        ks = slice(2 * u, 2 * u + 2)
                        ps = bank[:, :].rearrange("p (k s) -> p k s", k=2)
                        chain.did(V.scalar_tensor_tensor(out=a.CN[:, ks, :], in0=ps, scalar=1.0 / WS, in1=a.CN[:, ks, :],
                                                         op0=ALU.mult, op1=ALU.add))
                        chain.wait(dve)
                        dve.sem_inc(a.proj_out, 1)
                        hi = g.XTh[:, ks, bass.ds(n.idx * S0, S0)]
                        lo = g.XTl[:, ks, bass.ds(n.idx * S0, S0)]
                        chain.did(V.tensor_copy(hi, a.CN[:, ks, :]))
                        chain.wait(dve)
                        chain.did(V.tensor_tensor(lo, a.CN[:, ks, :], hi, ALU.subtract))

                PRE, POST = 7 + 2 + 8, 4 + 6
                b0, b1 = Batch(0, 0), Batch(0, 1)
                uses, chain = Uses(0, 0), Chain(a.dve_step, 0)
                pre_qkv(b0, uses, chain)
                pre_norm(b0, uses, chain)
                pre_qk(b0, uses, chain)
                for s in range(c.slots):
                    a.dve_max(dve, b0, s)
                a.dve_shift(dve, b0, uses)
                pre_qkv(b1, uses, chain)
                pre_norm(b1, uses, chain)
                pre_qk(b1, uses, chain)
                assert chain.n == 2 * PRE

                def step(b, b1, b2, uses, chain):
                    if b1 is not None:
                        for s in range(c.slots):
                            a.dve_max(dve, b1, s)
                        a.dve_shift(dve, b1, uses)
                    if b2 is not None:
                        pre_qkv(b2, uses, chain)
                        pre_norm(b2, uses, chain)
                    post(b, uses, chain)
                    if b2 is not None:
                        pre_qk(b2, uses, chain)

                with dve.Fori(0, NB // 2 - 1) as i:
                    for q in range(2):
                        b = Batch(i, q)
                        chain = Chain(a.dve_step, 2 * PRE + (PRE + POST) * b.idx)
                        step(b, Batch(i, q + 1), Batch(i, q + 2), c.uses_at(b, q), chain)
                        assert chain.n == PRE + POST
                i = NB // 2 - 1
                b = Batch(i, 0)
                uses, chain = c.uses_at(b, 0), Chain(a.dve_step, 2 * PRE + (PRE + POST) * b.idx)
                step(b, Batch(i, 1), None, uses, chain)
                step(Batch(i, 1), None, None, uses, chain)


def layer1_experts(nc, g, Wg, Wu, Wd, Wr, Ag, Bg, Au, Bu, Ad, Bd, desc, out):
    LORA = 2.0
    CH = S0
    ER = E * R
    ITEMS = [(kind, f) for i in range(FT + 2) for kind, f in ((0, i), (1, i - 1), (2, i - 2)) if 0 <= f < FT]
    NI = len(ITEMS)
    NUM = {it: k for k, it in enumerate(ITEMS)}
    with ExitStack() as ctx:
        sb = lambda name, shape, dt: ctx.enter_context(nc.sbuf_tensor(f"d_{name}", shape, dt))
        sem = lambda name: ctx.enter_context(nc.semaphore(f"d_{name}"))
        bank = [ctx.enter_context(nc.psum_tensor(f"d_bank{i}", [P, 512], F32)) for i in range(8)]
        GU, O, Z = bank[0:4], bank[4:6], bank[6:8]
        two = lambda name, shape: (sb(name + "h", shape, F16), sb(name + "l", shape, F16))
        wg, wu, wd = two("wg", [P, KF, DFF]), two("wu", [P, KF, DFF]), two("wd", [P, FT, T0])
        bgu = two("bgu", [ER, 2, DFF])
        agu = two("agu", [P, 2, KF, ER])
        ad, bd = two("ad", [P, FT, ER]), two("bd", [ER, T0])
        wr = two("wr", [P, KF, E])
        r = Router(nc, ctx, "d")
        kinds = sb("kinds", [P, NT, 4, E], F32)
        EX = sb("EX", [P, 2, 4, E, R], F32)
        SG = [sb(f"SG{i}", [P, CH], F32) for i in range(3)]
        HF = sb("HF", [P, CH], F32)
        HS = [[two(f"H{kind}{i}_", [P, CH]) for i in range(2)] for kind in range(3)]
        al = two("al", [ER, 2, CH])
        M = [two(f"M{i}", [ER, 2, CH]) for i in range(2)]
        MK = sb("MK", [ER, 2, CH], F16)
        MW = sb("MW", [ER, 2, CH], F32)
        ZZ = sb("ZZ", [ER, 2, CH], F32)
        zz = two("zz", [ER, CH])
        Y = [sb(f"Y{i}", [P, T0], F32) for i in range(2)]
        step_sem = sem("dve_step")

        with ExitStack() as setup:
            tmp = lambda name, shape: setup.enter_context(nc.sbuf_tensor(f"ds_{name}", shape, F32))
            sg, su = ([tmp(f"{n}{i}", [P, T0]) for i in range(2)] for n in ("sg", "su"))
            sd = [tmp(f"sd{i}", [P, KF, P]) for i in range(2)]
            sbg, sbu = ([tmp(f"{n}{i}", [P, E, R]) for i in range(2)] for n in ("sbg", "sbu"))
            sa = [tmp(f"sa{i}", [ER, P]) for i in range(2)]
            first_in = sem("first_in")
            t_in = [sem("t_in0"), sem("t_in1")]
            turned, hi_done, lo_done = sem("turned"), sem("hi_done"), sem("lo_done")
            first_hi, first_lo = sem("first_hi"), sem("first_lo")
            logits, routed, exped = sem("logits"), sem("routed"), sem("exped")
            fa, fu = Y[0], Y[1]
            fb = ZZ[:, :, :].rearrange("p a c -> p (a c)").rearrange("p (t e r) -> p t e r", t=KF, e=E)
            fr = EX[0:E, 0, :, :, :].rearrange("p k e r -> p (k e r)")

            def each_tile(eng, step):
                with eng.Fori(0, FT // 2) as i:
                    for q in range(2):
                        step(Batch(i, q))
                step(Batch(FT // 2, 0))

            def outputs(n):
                b = bank[4 * n.par:4 * n.par + 4]
                cols = bass.ds(n.idx * P, P)
                v = lambda x: x[:, :].rearrange("p (k c) -> p k c", k=KF)
                return [(v(b[0]), wg, lambda w: w[:, :, cols], WS), (v(b[1]), wu, lambda w: w[:, :, cols], WS),
                        (b[2][:, :], wd, lambda w: w[:, n.idx, :], WS),
                        (b[3][:, 0:2 * P].rearrange("p (w c) -> p w c", w=2), bgu, lambda w: w[:, :, cols], LORA * WS),
                        (b[3][:, 2 * P:3 * P], ad, lambda w: w[:, n.idx, :], WS)]

            v4 = lambda x: x[:, :].rearrange("p (k c) -> p k c", k=KF)
            firsts = [(v4(bank[0]), agu, lambda w: w[:, 0, :, :], WS), (v4(bank[1]), agu, lambda w: w[:, 1, :, :], WS),
                      (bank[2][:, :], bd, lambda w: w[:, :], LORA * WS),
                      (bank[3][:, 0:KF * E].rearrange("p (k e) -> p k e", k=KF), wr, lambda w: w[:, :, :], WS)]

            with nc.Block() as block:
                @block.sync
                def _(sp):
                    sp.dma_start(fa[:, :], Ag.rearrange("e r f -> (e r) f")).then_inc(first_in, 16)
                    sp.dma_start(fu[:, :], Au.rearrange("e r f -> (e r) f")).then_inc(first_in, 16)
                    sp.dma_start(fr, Wr).then_inc(first_in, 16)
                    for k in range(KF):
                        sp.dma_start(fb[:, k, :, :], Bd[:, k * P:(k + 1) * P, :].rearrange("e p r -> p e r")).then_inc(first_in, 16)
                    sp.dma_start(r.desc[:, :, :], desc).then_inc(first_in, 16)

                    def load(n):
                        rows = bass.ds(n.idx * P, P)
                        if not (isinstance(n.idx, int) and n.idx < 2):
                            sp.wait_ge(turned, n.idx - 1 + 1)
                        sp.dma_start(sg[n.par][:, :], Wg[rows, :]).then_inc(t_in[n.par], 16)
                        sp.dma_start(su[n.par][:, :], Wu[rows, :]).then_inc(t_in[n.par], 16)
                        sp.dma_start(sd[n.par][:, :, :], Wd[:, rows].rearrange("(k p) c -> p k c", p=P)).then_inc(t_in[n.par], 16)
                        sp.dma_start(sbg[n.par][:, :, :], Bg[:, rows, :].rearrange("e p r -> p e r")).then_inc(t_in[n.par], 16)
                        sp.dma_start(sbu[n.par][:, :, :], Bu[:, rows, :].rearrange("e p r -> p e r")).then_inc(t_in[n.par], 16)
                        sp.dma_start(sa[n.par][:, :], Ad.rearrange("e r c -> (e r) c")[:, rows]).then_inc(t_in[n.par], 16)

                    load(Batch(0, 0))
                    load(Batch(0, 1))
                    with sp.Fori(1, FT // 2) as i:
                        for q in range(2):
                            load(Batch(i, q))
                    load(Batch(FT // 2, 0))

                @block.tensor
                def _(pe):
                    T = nc.tensor.transpose
                    pe.wait_ge(first_in, 16 * 8)
                    for k in range(KF):
                        T(bank[0][:, k * P:(k + 1) * P], fa[:, k * P:(k + 1) * P], g.ident[:, :])
                        T(bank[1][:, k * P:(k + 1) * P], fu[:, k * P:(k + 1) * P], g.ident[:, :])
                        T(bank[2][:, k * P:(k + 1) * P], fb[:, k, :, :].rearrange("p e r -> p (e r)"), g.ident[:, :])
                        mm = T(bank[3][:, k * E:(k + 1) * E], fr[:, k * P:(k + 1) * P], g.ident[0:E, 0:E])
                    mm.then_inc(turned, 1)
                    pe.wait_ge(first_lo, 1)

                    def step(n):
                        pe.wait_ge(t_in[n.par], 96 * (n.half + 1))
                        pe.wait_ge(lo_done, n.idx + 1)
                        b = bank[4 * n.par:4 * n.par + 4]
                        for k in range(KF):
                            ks = slice(k * P, (k + 1) * P)
                            T(b[0][:, ks], sg[n.par][:, ks], g.ident[:, :])
                            T(b[1][:, ks], su[n.par][:, ks], g.ident[:, :])
                            T(b[2][:, ks], sd[n.par][:, k, :], g.ident[:, :])
                        T(b[3][:, 0:P], sbg[n.par][:, :, :].rearrange("p e r -> p (e r)"), g.ident[:, :])
                        T(b[3][:, P:2 * P], sbu[n.par][:, :, :].rearrange("p e r -> p (e r)"), g.ident[:, :])
                        T(b[3][:, 2 * P:3 * P], sa[n.par][:, :], g.ident[:, :]).then_inc(turned, 1)

                    each_tile(pe, step)
                    pe.wait_ge(lo_done, FT + 2)
                    for t in range(NT):
                        n = 0
                        for k in range(KF):
                            for xs, ws in ((g.XTh, wr[0]), (g.XTl, wr[0]), (g.XTh, wr[1])):
                                mm = nc.tensor.matmul(bank[7][:, t * E:(t + 1) * E], xs[:, k, t * P:(t + 1) * P], ws[:, k, :],
                                                      start=(n == 0), stop=(n == 3 * KF - 1))
                                n += 1
                    mm.then_inc(logits, 1)

                @block.scalar
                def _(act):
                    act.wait_ge(turned, 1)
                    for src, w, dst, scale in firsts:
                        ins = nc.scalar.activation(dst(w[0]), src, ACT.Copy, scale=scale)
                    ins.then_inc(first_hi, 1)

                    def step(n):
                        act.wait_ge(turned, n.idx + 2)
                        for src, w, dst, scale in outputs(n):
                            ins = nc.scalar.activation(dst(w[0]), src, ACT.Copy, scale=scale)
                        ins.then_inc(hi_done, 1)

                    each_tile(act, step)
                    act.wait_ge(routed, 1)
                    nc.scalar.activation(r.ex[:, :, :], r.t[:, :, :], ACT.Exp)
                    nc.scalar.activation(r.w2[:, :], r.s[:, :], ACT.Exp).then_inc(exped, 1)

                @block.vector
                def _(dve):
                    V = nc.vector
                    chain = Chain(step_sem)

                    def did(ins):
                        chain.did(ins)
                        chain.wait(dve)

                    dve.sem_inc(lo_done, 2)
                    dve.wait_ge(first_hi, 1)
                    for src, w, dst, scale in firsts:
                        ins = V.scalar_tensor_tensor(out=dst(w[1]), in0=src, scalar=scale, in1=dst(w[0]),
                                                     op0=ALU.mult, op1=ALU.subtract)
                    ins.then_inc(first_lo, 1)

                    def step(n):
                        dve.wait_ge(hi_done, n.idx + 1)
                        for src, w, dst, scale in outputs(n):
                            ins = V.scalar_tensor_tensor(out=dst(w[1]), in0=src, scalar=scale, in1=dst(w[0]),
                                                         op0=ALU.mult, op1=ALU.subtract)
                        ins.then_inc(lo_done, 1)

                    each_tile(dve, step)
                    dve.wait_ge(logits, 1)
                    route_vector(nc, dve, r, bank[7][:, 0:NT * E].rearrange("p (t e) -> p t e", t=NT), chain)
                    over = lambda ap: ap.unsqueeze(2).to_broadcast([P, NT, E])
                    did(V.tensor_tensor(r.s[:, :], r.m2[:, :], r.m1[:, :], ALU.subtract))
                    did(V.tensor_tensor(r.t[:, :, :], r.l[:, :, :], over(r.m1[:, :]), ALU.subtract))
                    dve.sem_inc(routed, 1)
                    dve.wait_ge(exped, 1)
                    did(V.tensor_reduce(r.w1[:, :], r.ex[:, :, :], AX, ALU.add))
                    did(V.reciprocal(r.w1[:, :], r.w1[:, :]))
                    did(V.tensor_scalar(r.w1[:, :], r.w1[:, :], 1.0 / WS, None, ALU.mult))
                    did(V.tensor_tensor(r.w2[:, :], r.w2[:, :], r.w1[:, :], ALU.mult))
                    did(V.tensor_copy(kinds[:, :, 0, :], r.oh1[:, :, :]))
                    did(V.tensor_tensor(kinds[:, :, 1, :], r.oh2[:, :, :], r.oh1[:, :, :], ALU.subtract))
                    did(V.tensor_tensor(kinds[:, :, 2, :], r.oh1[:, :, :], over(r.w1[:, :]), ALU.mult))
                    did(V.tensor_tensor(kinds[:, :, 3, :], r.oh2[:, :, :], over(r.w2[:, :]), ALU.mult))

        ex_done, ex_begun, a_made, masks_made = sem("ex_done"), sem("ex_begun"), sem("a_made"), sem("masks_made")
        pre_step = sem("pre_step")
        made, silu, mult, hid = sem("made"), sem("silu"), sem("mult"), sem("hid")
        used = [sem("used0"), sem("used1"), sem("used2")]
        z_made, z_split, o_made, y_done = sem("z_made"), sem("z_split"), sem("o_made"), sem("y_done")
        y_out = [sem("y_out0"), sem("y_out1")]
        hi_step = sem("hi_step")

        with nc.Block() as block:
            @block.sync
            def _(sp):
                for t in range(2):
                    sp.sem_inc(y_out[t], 1)
                with sp.Fori(0, NB) as n:
                    for t in range(2):
                        sp.wait_ge(y_done, 2 * n + t + 2)
                        sp.dma_start(out[n, t * P:(t + 1) * P, :], Y[t][:, :]).then_inc(y_out[t], 16)
                for t in range(2):
                    sp.wait_ge(y_out[t], 16 * NB + 1)

            @block.gpsimd
            def _(pool):
                with pool.Fori(0, NB) as n:
                    pool.wait_ge(masks_made, n + 1)
                    pool.sem_inc(ex_begun, 1)
                    src = kinds[:, bass.ds(2 * n, 2), :, :].rearrange("p t k e -> p (t k e)").unsqueeze(2).to_broadcast([P, 2 * 4 * E, R])
                    nc.gpsimd.tensor_copy(EX[:, :, :, :, :].rearrange("p t k e r -> p (t k e) r"), src).then_inc(ex_done, 1)

            @block.tensor
            def _(pe):
                MM = nc.tensor.matmul

                passes = ((0, 0), (0, 1), (1, 0))

                with pe.Fori(0, NB) as n:
                    toks = bass.ds(n * CH, CH)
                    X = (g.XTh, g.XTl)
                    pe.wait_ge(mult, NI * n + 3)
                    for w in range(2):
                        for k in range(KF):
                            for i, (s, m) in enumerate(passes):
                                mm = MM(GU[0][:, w * CH:(w + 1) * CH], agu[s][:, w, k, :], X[m][:, k, toks],
                                        start=(k == 0 and i == 0), stop=(k == KF - 1 and i == 2))
                    mm.then_inc(a_made, 1)
                    pe.wait_ge(ex_done, n + 1)
                    for kind in range(4):
                        for t in range(2):
                            mm = nc.tensor.transpose(GU[1 + kind // 2][:, kind % 2 * CH + t * P:kind % 2 * CH + (t + 1) * P],
                                                     EX[:, t, kind, :, :].rearrange("p e r -> p (e r)"), g.ident[:, :])
                    mm.then_inc(masks_made, 1)

                    def base(f):
                        if f == 1 or f == 2:
                            pe.wait_ge(pre_step, 8 * n + 2 * f)
                        if f >= 4:
                            pe.wait_ge(mult, NI * n + NUM[2, f - 4] + 4)
                        b = GU[(f + 3) % 4]
                        for w, wt in enumerate((wg, wu)):
                            for k in range(KF):
                                for i, (s, m) in enumerate(passes):
                                    mm = MM(b[:, w * CH:(w + 1) * CH], wt[s][:, k, f * P:(f + 1) * P], X[m][:, k, toks],
                                            start=(w == 0 and k == 0 and i == 0), stop=(k == KF - 1 and i == 2),
                                            skip_group_check=True)
                        mm.then_inc(made, 1)

                    def slot(kind, f):
                        if f == 0:
                            pe.wait_ge(pre_step, 8 * n + 4 + 2 * kind)
                        pe.wait_ge(mult, NI * n + NUM[kind - 1, f] + 4)
                        b = GU[(f + 3) % 4]
                        for w in range(2):
                            for i, (s, m) in enumerate(passes):
                                mm = MM(b[:, w * CH:(w + 1) * CH], bgu[s][:, w, f * P:(f + 1) * P], M[kind - 1][m][:, w, :],
                                        start=False, stop=(i == 2), skip_group_check=True)
                        mm.then_inc(made, 1)

                    def down(f):
                        if f == 0:
                            pe.wait_ge(y_done, 2 * n + 1)
                        pe.wait_ge(hid, NI * n + NUM[0, f] + 2)
                        H = HS[0][f % 2]
                        for t in range(2):
                            for i, (s, m) in enumerate(passes):
                                mm = MM(O[t][:, :], H[s][:, t * P:(t + 1) * P], wd[m][:, f, :],
                                        start=(f == 0 and i == 0), stop=False, skip_group_check=True)
                        mm.then_inc(used[0], 1)

                    def z(kind, f):
                        if f == 0:
                            pe.wait_ge(z_split, n + 1)
                        pe.wait_ge(hid, NI * n + NUM[kind, f] + 2)
                        H = HS[kind][f % 2]
                        for i, (s, m) in enumerate(passes):
                            mm = MM(Z[kind - 1][:, 0:CH], ad[s][:, f, :], H[m][:, :],
                                    start=(f == 0 and i == 0), stop=(f == FT - 1 and i == 2))
                        mm.then_inc(used[kind], 1)

                    for i in range(FT + 3):
                        if i < FT:
                            base(i)
                        if 0 <= i - 1 < FT:
                            slot(1, i - 1)
                        if 0 <= i - 2 < FT:
                            slot(2, i - 2)
                        if 0 <= i - 1 < FT:
                            down(i - 1)
                        if 0 <= i - 2 < FT:
                            z(1, i - 2)
                        if 0 <= i - 3 < FT:
                            z(2, i - 3)
                    pe.wait_ge(z_split, n + 2)
                    for t in range(2):
                        for i, (s, m) in enumerate(passes):
                            mm = MM(O[t][:, :], zz[s][:, t * P:(t + 1) * P], bd[m][:, :], start=False, stop=(i == 2),
                                    skip_group_check=True)
                        mm.then_inc(o_made, 1)

            @block.scalar
            def _(act):
                with act.Fori(0, NB) as n:
                    for k, (kind, f) in enumerate(ITEMS):
                        act.wait_ge(mult, NI * n + k + 1)
                        act.wait_ge(made, NI * n + k + 1)
                        nc.scalar.activation(SG[k % 3][:, :], GU[(f + 3) % 4][:, 0:CH], ACT.Silu, scale=1.0 / WS).then_inc(silu, 1)

            @block.vector
            def _(dve):
                V = nc.vector
                dve.sem_inc(mult, 3)
                dve.sem_inc(hid, 1)
                dve.sem_inc(masks_made, 1)
                dve.sem_inc(z_split, 1)
                dve.sem_inc(y_done, 1)
                for u in used:
                    dve.sem_inc(u, 1)
                with dve.Fori(0, NB) as n:
                    def pre(k, ins):
                        ins.then_inc(pre_step, 1)

                    gu = lambda b: b[:, :].rearrange("p (w c) -> p w c", w=2)
                    dve.wait_ge(a_made, n + 1)
                    pre(1, V.tensor_scalar(al[0][:, :, :], gu(GU[0]), 1.0 / WS, None, ALU.mult))
                    dve.wait_ge(pre_step, 8 * n + 1)
                    pre(2, V.scalar_tensor_tensor(out=al[1][:, :, :], in0=gu(GU[0]), scalar=1.0 / WS, in1=al[0][:, :, :],
                                                  op0=ALU.mult, op1=ALU.subtract))
                    dve.wait_ge(masks_made, n + 2)
                    pre(3, V.tensor_copy(MK[:, :, :], gu(GU[1])))
                    pre(4, V.tensor_copy(MW[:, :, :], gu(GU[2])))
                    dve.wait_ge(pre_step, 8 * n + 4)
                    for i in range(2):
                        for h in range(2):
                            pre(5 + 2 * i + h, V.tensor_tensor(M[i][h][:, :, :], al[h][:, :, :],
                                                               MK[:, i, :].unsqueeze(1).to_broadcast([ER, 2, CH]), ALU.mult))
                    for k, (kind, f) in enumerate(ITEMS):
                        b = GU[(f + 3) % 4]
                        dve.wait_ge(silu, NI * n + k + 1)
                        dve.wait_ge(hid, NI * n + k + 1)
                        V.scalar_tensor_tensor(out=HF[:, :], in0=b[:, CH:2 * CH], scalar=1.0 / WS, in1=SG[k % 3][:, :],
                                               op0=ALU.mult, op1=ALU.mult).then_inc(mult, 1)
                        dve.wait_ge(mult, NI * n + k + 4)
                        dve.wait_ge(used[kind], FT * n + max(0, f - 1) + 1)
                        H = HS[kind][f % 2]
                        V.tensor_copy(H[0][:, :], HF[:, :]).then_inc(hi_step, 1)
                        dve.wait_ge(hi_step, (NI + 1) * n + k + 1)
                        V.tensor_tensor(H[1][:, :], HF[:, :], H[0][:, :], ALU.subtract).then_inc(hid, 1)
                    dve.wait_ge(used[2], FT * (n + 1) + 1)
                    V.tensor_tensor(ZZ[:, 0, :], Z[0][:, 0:CH], MW[:, 0, :], ALU.mult).then_inc(z_made, 1)
                    V.tensor_tensor(ZZ[:, 1, :], Z[1][:, 0:CH], MW[:, 1, :], ALU.mult).then_inc(z_made, 1)
                    dve.wait_ge(z_made, 3 * n + 2)
                    V.tensor_tensor(ZZ[:, 0, :], ZZ[:, 0, :], ZZ[:, 1, :], ALU.add).then_inc(z_made, 1)
                    dve.wait_ge(z_made, 3 * n + 3)
                    V.tensor_copy(zz[0][:, :], ZZ[:, 0, :]).then_inc(hi_step, 1)
                    dve.wait_ge(hi_step, (NI + 1) * (n + 1))
                    V.tensor_tensor(zz[1][:, :], ZZ[:, 0, :], zz[0][:, :], ALU.subtract).then_inc(z_split, 1)
                    for t in range(2):
                        dve.wait_ge(o_made, 2 * n + t + 1)
                        dve.wait_ge(y_out[t], 16 * n + 1)
                        V.scalar_tensor_tensor(out=Y[t][:, :], in0=O[t][:, :], scalar=1.0 / WS, in1=g.x1[:, 2 * n + t, :],
                                               op0=ALU.mult, op1=ALU.add).then_inc(y_done, 1)


class Lasting:
    pass


def build(nc, ins, consts, out):
    with ExitStack() as ctx:
        sb = lambda name, shape, dt: ctx.enter_context(nc.sbuf_tensor(name, shape, dt))
        sem = lambda name: ctx.enter_context(nc.semaphore(name))
        g = Lasting()
        g.ident = sb("ident", [P, P], F32)
        g.x1 = sb("x1", [P, NT, T0], F32)
        g.XTh = sb("XTh", [P, KF, NB * S0], F16)
        g.XTl = sb("XTl", [P, KF, NB * S0], F16)
        g.x1_in, g.ident_set = sem("x1_in"), sem("ident_set")
        with nc.Block() as block:
            @block.gpsimd
            def _(pool):
                nc.gpsimd.memset(g.ident[:, :], 0.0).then_inc(g.ident_set, 1)
                pool.wait_ge(g.ident_set, 1)
                nc.gpsimd.affine_select(out=g.ident[:, :], in_=g.ident[:, :], compare_op=ALU.not_equal, fill=1.0,
                                        base=0, pattern=[[-1, P]], channel_multiplier=1).then_inc(g.ident_set, 1)
        layer0_attention(nc, g, ins["x"], ins["cond_2048"], ins["L0_cond_Wq"], ins["L0_cond_Wo"], consts["sel0"])
        layer0_experts(nc, g, ins["L0_ffn_w_router"], ins["L0_ffn_w_gate"], ins["L0_ffn_w_up"],
                       ins["L0_ffn_w_down"], consts["desc"])
        layer1_attention(nc, g, ins["cond_2048"], ins["L1_cond_W_emb"], ins["L1_cond_b_emb"], ins["L1_cond_g_norm"],
                         ins["L1_cond_W_qkv"], ins["L1_cond_g_q"], ins["L1_cond_g_k"], ins["L1_cond_W_out"], consts["sel1"])
        layer1_experts(nc, g, *(ins["L1_ffn_" + n] for n in ("Wg", "Wu", "Wd", "Wr", "Ag", "Bg", "Au", "Bu", "Ad", "Bd")),
                       consts["desc"], out)


def selection(heads):
    import numpy as np
    s = np.zeros((heads, heads // 4, P), np.float32)
    for h in range(heads):
        s[(h % 2) * (heads // 2) + h // 2, h // 4, 32 * (h % 4):32 * (h % 4) + 32] = 1.0
    return s


def descending():
    import numpy as np
    return np.broadcast_to(np.arange(E, 0, -1, dtype=np.float32), (P, NT, E)).copy()


def kernel(**inputs):
    import numpy as _np
    import concourse.bacc as _bacc
    from concourse import mybir as _mybir
    from concourse.bass_utils import run_bass_kernel_spmd as _run

    nc = _bacc.Bacc("TRN2", target_bir_lowering=False, num_devices=1)
    arrays, ins, consts = {}, {}, {}
    for name in inputs:
        a = _np.ascontiguousarray(inputs[name])
        arrays["in_" + name] = a
        ins[name] = nc.dram_tensor("in_" + name, a.shape, _mybir.dt.from_np(a.dtype), kind="ExternalInput").ap()
    for name, a in {"sel0": selection(8), "sel1": selection(16), "desc": descending()}.items():
        arrays["const_" + name] = a
        consts[name] = nc.dram_tensor("const_" + name, a.shape, F32, kind="ExternalInput").ap()
    out = nc.dram_tensor("out", (NB, S0, T0), F32, kind="ExternalOutput").ap()
    build(nc, ins, consts, out)
    return _run(nc, [arrays], core_ids=[0]).results[0]["out"]
```

```python
from contextlib import ExitStack

import concourse.bass as bass
from concourse import mybir

F32 = mybir.dt.float32
F32R = mybir.dt.float32r
F16 = mybir.dt.float16
ALU = mybir.AluOpType
ACT = mybir.ActivationFunctionType
AX = mybir.AxisListType.X

P = 128
NB = 8
S0 = 256
T0 = 512
KF = T0 // P
NT = NB * S0 // P
E = 8
F0 = 352
F0_TILES = [(0, 128), (128, 128), (256, 96)]
DFF = 1408
FT = DFF // P
R = 16
WS = 64.0
NEG = -1e30
BIG = 3e38


class Batch:

    def __init__(self, i, q):
        self.idx = 2 * i + q
        self.half = i + q // 2
        self.par = q % 2
        self.first = isinstance(i, int) and 2 * i + q == 0


class Uses:

    def __init__(self, base, parity):
        self.base, self.k, self.parity = base, 0, parity

    def take(self):
        idx, bank = self.base + self.k, (self.parity + self.k) % 2
        self.k += 1
        return idx, bank


class Core:

    def __init__(self, heads, n, n_pre, n_v, v_opening, mask_row, lag, dt):
        self.heads, self.n = heads, n
        self.tiles = n // P
        self.kps = 512 // n
        self.sph = self.tiles // self.kps
        self.slots = heads * self.sph
        self.pairs = heads // 2
        self.groups = heads // 4
        self.k_nat = 97 if mask_row else 96
        self.k_t = self.k_nat + 1
        self.lag = lag
        self.dt = dt
        self.base0 = 2 * n_pre + v_opening * n_v + 1
        self.uses = n_pre + n_v + 1 + 4

    def uses_at(self, b, q):
        return Uses(self.base0 + self.uses * b.idx, (self.base0 + self.uses * q) % 2)

    def plan(self, cut, mids, ends):
        parts = [("first",)], []
        after = {}
        for j in range(self.slots):
            after.setdefault(self.lag + j * (self.slots - self.lag) // self.slots, []).append(("nat", j))
        for s in range(self.slots):
            parts[s >= cut].extend([("slot", s)] + after.get(s, []) + [(m,) for m in mids.get(s, ())])
        parts[1].extend((m,) for m in ends)
        return parts


def walk(plan, table, b=None, b1=None, b2=None, last=None):
    batch = {"first": b, "slot": b, "nat": b1, "shift": b1, "recip": last, "spread": last, "out": last}
    for name, *args in plan:
        n = batch.get(name, b1 if name[0] == "v" else b2)
        if n is not None and name in table:
            table[name](n, *args)


def plain(ap):
    return ap.bitcast(F32) if ap.dtype == F32R else ap


class Attention:

    def __init__(self, nc, ctx, tag, core, ident):
        self.nc, self.c, self.ident = nc, core, ident
        c = core
        sb = lambda name, shape, dt: ctx.enter_context(nc.sbuf_tensor(f"{tag}_{name}", shape, dt))
        ps = lambda name: ctx.enter_context(nc.psum_tensor(f"{tag}_{name}", [P, 512], F32))
        sem = lambda name: ctx.enter_context(nc.semaphore(f"{tag}_{name}"))
        self.A = [sb(f"A{i}", [c.k_t, c.heads, c.n], c.dt) for i in range(2)]
        self.B = [sb(f"B{i}", [c.k_t, c.heads, c.n], c.dt) for i in range(2)]
        self.V = [sb(f"V{i}", [P, c.tiles, c.heads, 64], F32) for i in range(2)]
        self.EX = [sb(f"EX{i}", [P, 512], F32) for i in range(4)]
        self.CS = sb("CS", [P, c.pairs, c.n], F32)
        self.CT = sb("CT", [P, c.groups, c.n], F32)
        self.RR = sb("RR", [c.heads, c.n], F32)
        self.RV = sb("RV", [c.heads, c.n], F32)
        self.NM = sb("NM", [P, c.heads * c.tiles], F32)
        self.SR = sb("SR", [c.heads * c.tiles, P], c.dt)
        self.SEL = sb("SEL", [c.heads, c.groups, P], F32)
        self.bn = [ps(f"bn{i}") for i in range(2)]
        self.bt = [ps(f"bt{i}") for i in range(2)]
        self.bc = [ps(f"bc{i}") for i in range(2)]
        self.pp = [ps(f"pp{i}") for i in range(2)]
        self.nat_made = sem("nat_made")
        self.max_done = sem("max_done")
        self.st_made = sem("st_made")
        self.exp_done = sem("exp_done")
        self.pv_done = sem("pv_done")
        self.ctx_out = sem("ctx_out")
        self.proj_made = sem("proj_made")
        self.proj_out = sem("proj_out")
        self.shift_rows = sem("shift_rows")
        self.shift_in = sem("shift_in")
        self.split_done = sem("split_done")
        self.a_in = sem("a_in")
        self.b_in = sem("b_in")
        self.may_assemble = sem("may_assemble")
        self.v_ready = sem("v_ready")
        self.ctx_in = sem("ctx_in")
        self.recip_done = sem("recip_done")
        self.ctx_norm = sem("ctx_norm")
        self.post_done = sem("post_done")
        self.dve_step = sem("dve_step")

    AB_DMAS = 12
    CTX_DMAS = 6

    def assemble(self, sp, n, dst, done, parts):
        sp.wait_ge(self.split_done, n.idx + 1)
        if not n.first:
            sp.wait_ge(self.st_made, self.c.slots * (n.idx - 1) + 1)
        sp.sem_inc(self.may_assemble, 1)
        for j in range(4):
            for r, src in enumerate(parts):
                sp.dma_start(plain(dst[n.par][32 * r:32 * r + 32, j::4, :]),
                             plain(src[32 * j:32 * j + 32, :, :])).then_inc(done, 16)

    def act_shift(self, act, n):
        c = self.c
        act.wait_ge(self.shift_rows, n.idx + 1)
        dst = self.A[n.par][c.k_nat:c.k_t, :, :].rearrange("p h (t j) -> p (h t) j", j=P)
        act.dma_start(plain(dst), plain(self.SR[:, :])).then_inc(self.shift_in, 16)

    def sp_context(self, sp, n):
        c = self.c
        sp.wait_ge(self.ctx_out, c.pairs * (n.idx + 1) + 2)
        sp.wait_ge(self.post_done, n.idx + 1)
        for j in range(4):
            src = self.CS[64 * (j % 2):64 * (j % 2) + 32, j // 2::2, :]
            sp.dma_start(self.CT[32 * j:32 * j + 32, :, :], src).then_inc(self.ctx_in, 16)
        for odd in range(2):
            sp.dma_start(self.RR[odd * c.pairs:(odd + 1) * c.pairs, :],
                         self.CS[32 + 64 * odd:33 + 64 * odd, :, :]).then_inc(self.ctx_in, 16)

    def pe_take(self, pe, uses):
        idx, bank = uses.take()
        pe.wait_ge(self.proj_out, idx + 1)
        return self.pp[bank]

    def pe_nat(self, pe, n, s):
        c, nc = self.c, self.nc
        if s == 0:
            pe.wait_ge(self.a_in, 16 * self.AB_DMAS * (n.idx + 1))
            pe.wait_ge(self.b_in, 16 * self.AB_DMAS * (n.idx + 1))
        pe.wait_ge(self.max_done, c.slots * n.idx + s + 1)
        h, t0 = s // c.sph, (s % c.sph) * c.kps
        A, B = self.A[n.par], self.B[n.par]
        for k in range(c.kps):
            mm = nc.tensor.matmul(self.bn[s % 2][:, k * c.n:(k + 1) * c.n],
                                  A[0:c.k_nat, h, (t0 + k) * P:(t0 + k + 1) * P],
                                  B[0:c.k_nat, h, :], start=True, stop=True)
        mm.then_inc(self.nat_made, 1)

    def pe_shift(self, pe, n, uses):
        c = self.c
        pe.wait_ge(self.max_done, c.slots * (n.idx + 1) + 2)
        bank = self.pe_take(pe, uses)
        self.nc.tensor.transpose(bank[0:c.heads * c.tiles, 0:P], self.NM[:, :], self.ident[:, :]).then_inc(self.proj_made, 1)

    def pe_st(self, pe, n, s):
        c, nc = self.c, self.nc
        if s == 0:
            pe.wait_ge(self.shift_in, 16 * (n.idx + 1))
        pe.wait_ge(self.exp_done, c.slots * n.idx + s + 1)
        h, t0 = s // c.sph, (s % c.sph) * c.kps
        A, B = self.A[n.par], self.B[n.par]
        for k in range(c.kps):
            mm = nc.tensor.matmul(self.bt[s % 2][:, k * c.n:(k + 1) * c.n],
                                  B[0:c.k_t, h, (t0 + k) * P:(t0 + k + 1) * P],
                                  A[0:c.k_t, h, :], start=True, stop=True)
        mm.then_inc(self.st_made, 1)

    def pe_pv(self, pe, n, s):
        c, nc = self.c, self.nc
        if s == 0:
            pe.wait_ge(self.v_ready, n.idx + 1)
        h, t0 = s // c.sph, (s % c.sph) * c.kps
        if h % 2 == 0 and t0 == 0:
            pe.wait_ge(self.ctx_out, c.pairs * n.idx + h // 2 + 1)
        pe.wait_ge(self.exp_done, c.slots * n.idx + s + 3)
        half = 64 * (h % 2)
        for k in range(c.kps):
            t = t0 + k
            mm = nc.tensor.matmul(self.bc[h // 2 % 2][half:half + 64, 0:c.n], self.V[n.par][:, t, h, :],
                                  self.EX[s % 4][:, k * c.n:(k + 1) * c.n],
                                  start=(t == 0), stop=(t == c.tiles - 1), tile_position=(0, half))
        mm.then_inc(self.pv_done, 1)

    def pe_spread(self, pe, n, uses):
        c, nc = self.c, self.nc
        pe.wait_ge(self.recip_done, n.idx + 1)
        for u in range(2):
            bank = self.pe_take(pe, uses)
            for k in range(c.kps):
                mm = nc.tensor.matmul(bank[:, k * c.n:(k + 1) * c.n], self.SEL[:, u * c.kps + k, :],
                                      self.RV[:, :], start=True, stop=True)
            mm.then_inc(self.proj_made, 1)

    def pe_first(self, pe, b):
        self.pe_st(pe, b, 0)
        self.pe_st(pe, b, 1)

    def pe_slot(self, pe, b, s):
        if s + 2 < self.c.slots:
            self.pe_st(pe, b, s + 2)
        self.pe_pv(pe, b, s)

    def act_slot(self, act, b, s):
        c, nc = self.c, self.nc
        act.wait_ge(self.st_made, c.slots * b.idx + s + 2)
        act.wait_ge(self.pv_done, c.slots * b.idx + s + 1)
        nc.scalar.activation(self.EX[s % 4][:, :], self.bt[s % 2][:, :], ACT.Exp).then_inc(self.exp_done, 1)
        if s >= 2 and (s - 1) % (2 * c.sph) == 0:
            self.act_context(act, b, (s - 1) // (2 * c.sph) - 1)
        if s == c.slots - 1:
            self.act_context(act, b, c.pairs - 1)

    def act_context(self, act, b, pr):
        c = self.c
        if pr == 0:
            act.wait_ge(self.ctx_in, 16 * self.CTX_DMAS * b.idx + 1)
        act.wait_ge(self.pv_done, c.slots * b.idx + (pr + 1) * 2 * c.sph + 4)
        self.nc.scalar.copy(self.CS[:, pr, :], self.bc[pr % 2][:, 0:c.n]).then_inc(self.ctx_out, 1)

    def dve_max(self, dve, n, s):
        c = self.c
        dve.wait_ge(self.nat_made, c.slots * n.idx + s + 1)
        cols = c.kps
        self.nc.vector.tensor_reduce(self.NM[:, s * cols:(s + 1) * cols],
                                     self.bn[s % 2][:, :].rearrange("p (k n) -> p k n", k=cols),
                                     AX, ALU.max, negate=True).then_inc(self.max_done, 1)

    def taken(self, eng, uses):
        idx, bank = uses.take()
        eng.wait_ge(self.proj_made, idx + 1)
        return self.pp[bank]

    def dve_shift(self, dve, n, uses):
        c = self.c
        bank = self.taken(dve, uses)
        if not n.first:
            dve.wait_ge(self.shift_in, 16 * n.idx)
        self.nc.vector.tensor_copy(self.SR[:, :], bank[0:c.heads * c.tiles, 0:P]).then_inc(self.shift_rows, 1)
        dve.wait_ge(self.shift_rows, n.idx + 1)
        dve.sem_inc(self.proj_out, 1)

    def dve_recip(self, dve, n):
        dve.wait_ge(self.ctx_in, 16 * self.CTX_DMAS * (n.idx + 1) + 1)
        self.nc.vector.reciprocal(self.RV[:, :], self.RR[:, :]).then_inc(self.recip_done, 1)

    def prime(self, dve):
        dve.sem_inc(self.max_done, 2)
        dve.sem_inc(self.st_made, 1)
        dve.sem_inc(self.exp_done, 2)
        dve.sem_inc(self.pv_done, 4)
        dve.sem_inc(self.ctx_out, 2)
        dve.sem_inc(self.proj_out, 2)
        dve.sem_inc(self.ctx_in, 1)
        dve.sem_inc(self.post_done, 1)


def batches(eng, c, plan, pre, values, table, opening):
    head, rest = plan
    b0, b1 = Batch(0, 0), Batch(0, 1)
    walk([(m,) for m in pre + values], opening, b1=b0, b2=b0)
    walk([("nat", s) for s in range(c.slots)] + [("shift",)], opening, b1=b0)
    walk([(m,) for m in pre], opening, b2=b1)
    walk(head, opening, b0, b1)
    with eng.Fori(0, NB // 2 - 1) as i:
        for q in range(2):
            b = Batch(i, q)
            steps = table(b, q)
            walk(rest, steps, b, Batch(i, q + 1), Batch(i, q + 2))
            walk(head, steps, Batch(i, q + 1), Batch(i, q + 2), None, b)
    b, end = Batch(NB // 2 - 1, 0), Batch(NB // 2 - 1, 1)
    steps = table(b, 0)
    walk(rest, steps, b, end, None)
    walk(head, steps, end, None, None, b)
    walk(rest, steps, end, None, None)
    walk([("recip",), ("spread",), ("out",)], steps, last=end)


class Chain:

    def __init__(self, sem, base=0):
        self.sem, self.base, self.n = sem, base, 0

    def did(self, ins):
        ins.then_inc(self.sem, 1)
        self.n += 1

    def wait(self, eng):
        eng.wait_ge(self.sem, self.base + self.n)


def layer0_attention(nc, g, x, cond, wq, wo, sel):
    c = Core(heads=8, n=T0, n_pre=2, n_v=2, v_opening=1, mask_row=True, lag=10, dt=F32R)
    QSCALE = float((S0 // 8) ** -0.25)
    with ExitStack() as ctx:
        a = Attention(nc, ctx, "a0", c, g.ident)
        sb = lambda name, shape, dt: ctx.enter_context(nc.sbuf_tensor(f"a0_{name}", shape, dt))
        sem = lambda name: ctx.enter_context(nc.semaphore(f"a0_{name}"))
        xb = [sb(f"xb{i}", [P, 2, T0], F32) for i in range(2)]
        cb = [sb(f"cb{i}", [P, T0], F32) for i in range(2)]
        wn = sb("wn", [P, 2, 2, S0], F32)
        wT = sb("wT", [P, 2, 2, S0], F32)
        QM = sb("QM", [P, T0], F32)
        H = sb("H", [P, 2, T0], F32R)
        L = sb("L", [P, 2, T0], F32R)
        w_in, w_made, w_out = sem("w_in"), sem("w_made"), sem("w_out")
        x_in = [sem("x_in0"), sem("x_in1")]
        rows_done = sem("rows_done")
        MR = wn[0:1, :, :, :].rearrange("p a k d -> p a (k d)").bitcast(F32R)
        rows_begun = sem("rows_begun")
        rows_set = sem("rows_set")
        ones_set = sem("ones_set")

        pre, values_of = ("q0", "q1"), ("values",)
        plan = c.plan(14, {5: ("recip",), 9: ("spread",), 13: ("out",), 18: ("q0",), 25: ("q1",)}, ("shift", "values"))

        def over_batches(eng, table, opening):
            batches(eng, c, plan, pre, values_of, table, opening)

        with nc.Block() as block:
            def load(sp, n):
                if isinstance(n.idx, int) and n.idx < 2:
                    pass
                else:
                    sp.wait_ge(a.v_ready, n.idx - 1)
                    sp.wait_ge(rows_set, n.idx - 1)
                sp.dma_start(xb[n.par][:, :, :], x[n.idx].rearrange("(k p) t -> p k t", p=P)).then_inc(x_in[n.par], 16)
                sp.dma_start(cb[n.par][:, :], cond[bass.ds(n.idx, 1), :].to_broadcast([P, T0])).then_inc(x_in[n.par], 16)

            @block.sync
            def _(sp):
                for i, w in enumerate((wq, wo)):
                    sp.dma_start(wn[:, i, :, :], w.rearrange("(k p) d -> p k d", p=P)).then_inc(w_in, 16)
                sp.dma_start(a.SEL[:, :, :], sel).then_inc(w_in, 16)
                b0, b1 = Batch(0, 0), Batch(0, 1)
                load(sp, b0)
                load(sp, b1)
                sp.dma_start(g.x1[:, :, :], x.rearrange("b (t p) f -> p (b t) f", p=P)).then_inc(g.x1_in, 16)
                a.assemble(sp, b0, a.A, a.a_in, (H, L, H))
                a.assemble(sp, b1, a.A, a.a_in, (H, L, H))
                with sp.Fori(0, NB // 2 - 1) as i:
                    for q in range(2):
                        n = Batch(i, q + 2)
                        load(sp, n)
                        a.assemble(sp, n, a.A, a.a_in, (H, L, H))
                        a.sp_context(sp, Batch(i, q))
                a.sp_context(sp, Batch(NB // 2 - 1, 0))
                a.sp_context(sp, Batch(NB // 2 - 1, 1))
                sp.wait_ge(g.x1_in, 16)

            @block.gpsimd
            def _(pool):
                for k, buf in enumerate((a.B[0][96:98, :, :].bitcast(F32), a.B[1][96:98, :, :].bitcast(F32),
                                         a.V[0][:, :, :, :], a.V[1][:, :, :, :])):
                    nc.gpsimd.memset(buf, 1.0).then_inc(ones_set, 1)
                    pool.wait_ge(ones_set, k + 1)
                pool.wait_ge(w_out, 2)

                def rows(n):
                    a.assemble(pool, n, a.B, a.b_in, (H, H, L))
                    pool.wait_ge(x_in[n.par], 32 * (n.half + 1))
                    if not n.first:
                        pool.wait_ge(rows_done, 32 * n.idx)
                    pool.sem_inc(rows_begun, 1)
                    nc.gpsimd.tensor_copy(MR[:, 0, :], cb[n.par][0:1, :])
                    nc.gpsimd.tensor_scalar(MR[:, 1, :], cb[n.par][0:1, :], -NEG, NEG, ALU.mult, ALU.add).then_inc(rows_set, 1)
                    pool.wait_ge(rows_set, n.idx + 1)
                    pool.sem_inc(rows_begun, 1)
                    for i, dst in enumerate((a.A, a.B)):
                        pool.dma_start(plain(dst[n.par][96:97, :, :]),
                                       plain(MR[:, i, :]).unsqueeze(1).to_broadcast([1, c.heads, T0])).then_inc(rows_done, 16)

                rows(Batch(0, 0))
                rows(Batch(0, 1))
                with pool.Fori(0, NB // 2 - 1) as i:
                    for q in range(2):
                        rows(Batch(i, q + 2))

            @block.tensor
            def _(pe):
                pe.wait_ge(w_in, 48)
                pe.wait_ge(g.ident_set, 2)
                for i in range(2):
                    for k in range(2):
                        for o in range(2):
                            mm = nc.tensor.transpose(a.pp[i][:, k * 256 + o * P:k * 256 + (o + 1) * P],
                                                     wn[:, i, o, k * P:(k + 1) * P], g.ident[:, :])
                    mm.then_inc(w_made, 1)
                pe.wait_ge(w_out, 2)

                def q_tile(n, uses, o):
                    pe.wait_ge(x_in[n.par], 32 * (n.half + 1))
                    bank = a.pe_take(pe, uses)
                    for k in range(2):
                        mm = nc.tensor.matmul(bank[:, :], wT[:, 0, k, o * P:(o + 1) * P], xb[n.par][:, k, :],
                                              start=(k == 0), stop=(k == 1))
                    mm.then_inc(a.proj_made, 1)

                def values(n, uses):
                    for u in range(2):
                        bank = a.pe_take(pe, uses)
                        for t in range(2):
                            for k in range(2):
                                mm = nc.tensor.matmul(bank[:, t * S0:(t + 1) * S0],
                                                      xb[n.par][:, k, (2 * u + t) * P:(2 * u + t + 1) * P],
                                                      wT[:, 0, k, :], start=(k == 0), stop=(k == 1))
                        mm.then_inc(a.proj_made, 1)

                def out(n, uses):
                    pe.wait_ge(a.ctx_norm, 2 * (n.idx + 1))
                    for u in range(2):
                        bank = a.pe_take(pe, uses)
                        for t in range(2):
                            for k in range(2):
                                mm = nc.tensor.matmul(bank[:, t * S0:(t + 1) * S0],
                                                      a.CT[:, k, (2 * u + t) * P:(2 * u + t + 1) * P],
                                                      wT[:, 1, k, :], start=(k == 0), stop=(k == 1))
                        mm.then_inc(a.proj_made, 1)

                def nat(n, s):
                    if s == 0:
                        pe.wait_ge(rows_done, 32 * (n.idx + 1))
                    a.pe_nat(pe, n, s)

                def table(uses):
                    return {"first": lambda n: a.pe_first(pe, n), "slot": lambda n, s: a.pe_slot(pe, n, s),
                            "nat": nat, "shift": lambda n: a.pe_shift(pe, n, uses),
                            "q0": lambda n: q_tile(n, uses, 0), "q1": lambda n: q_tile(n, uses, 1),
                            "values": lambda n: values(n, uses),
                            "spread": lambda n: a.pe_spread(pe, n, uses), "out": lambda n: out(n, uses)}

                over_batches(pe, lambda b, q: table(c.uses_at(b, q)), table(Uses(0, 0)))

            @block.scalar
            def _(act):
                table = {"slot": lambda n, s: a.act_slot(act, n, s), "shift": lambda n: a.act_shift(act, n)}
                over_batches(act, lambda b, q: table, table)

            @block.vector
            def _(dve):
                a.prime(dve)
                for i in range(2):
                    dve.wait_ge(w_made, i + 1)
                    nc.vector.tensor_copy(wT[:, i, :, :], a.pp[i][:, :].rearrange("p (k o) -> p k o", k=2)).then_inc(w_out, 1)
                dve.wait_ge(ones_set, 4)

                steps = a.dve_step

                def q_tile(n, uses, chain, o):
                    bank = a.taken(dve, uses)
                    dve.wait_ge(x_in[n.par], 32 * (n.half + 1))
                    if o == 0 and not n.first:
                        dve.wait_ge(a.a_in, 16 * a.AB_DMAS * n.idx)
                        dve.wait_ge(a.b_in, 16 * a.AB_DMAS * n.idx)
                    chain.wait(dve)
                    chain.did(nc.vector.scalar_tensor_tensor(out=QM[:, :], in0=bank[:, :], scalar=QSCALE,
                                                             in1=cb[n.par][:, :], op0=ALU.mult, op1=ALU.mult))
                    chain.wait(dve)
                    dve.sem_inc(a.proj_out, 1)
                    chain.did(nc.vector.tensor_copy(H[:, o, :], QM[:, :]))
                    chain.wait(dve)
                    chain.did(nc.vector.tensor_tensor(L[:, o, :], QM[:, :], H[:, o, :].bitcast(F32), ALU.subtract))
                    if o == 1:
                        chain.wait(dve)
                        dve.sem_inc(a.split_done, 1)

                def values(n, uses):
                    for u in range(2):
                        bank = a.taken(dve, uses)
                        nc.vector.tensor_copy(a.V[n.par][:, 2 * u:2 * u + 2, :, 0:32],
                                              bank[:, :].rearrange("p (t h d) -> p t h d", t=2, h=c.heads)).then_inc(a.proj_out, 1)
                    dve.wait_ge(a.proj_out, uses.base + uses.k + 2)
                    dve.sem_inc(a.v_ready, 1)

                def spread(n, uses):
                    for u in range(2):
                        bank = a.taken(dve, uses)
                        nc.vector.tensor_tensor(a.CT[:, u, :], a.CT[:, u, :], bank[:, :], ALU.mult).then_inc(a.ctx_norm, 1)
                        dve.wait_ge(a.ctx_norm, 2 * n.idx + u + 1)
                        dve.sem_inc(a.proj_out, 1)

                def out(n, uses, chain):
                    for u in range(2):
                        bank = a.taken(dve, uses)
                        ps = bank[:, :].rearrange("p (t s) -> p t s", t=2)
                        hi = g.XTh[:, 2 * u:2 * u + 2, bass.ds(n.idx * S0, S0)]
                        lo = g.XTl[:, 2 * u:2 * u + 2, bass.ds(n.idx * S0, S0)]
                        chain.did(nc.vector.tensor_copy(hi, ps))
                        chain.wait(dve)
                        nc.vector.tensor_tensor(lo, ps, hi, ALU.subtract).then_inc(a.proj_out, 1)
                    dve.sem_inc(a.post_done, 1)

                PRE_STEPS, POST_STEPS = 6, 2

                def table(uses, chain):
                    return {"nat": lambda n, s: a.dve_max(dve, n, s), "shift": lambda n: a.dve_shift(dve, n, uses),
                            "q0": lambda n: q_tile(n, uses, chain, 0), "q1": lambda n: q_tile(n, uses, chain, 1),
                            "values": lambda n: values(n, uses),
                            "recip": lambda n: a.dve_recip(dve, n), "spread": lambda n: spread(n, uses),
                            "out": lambda n: out(n, uses, chain)}

                over_batches(dve, lambda b, q: table(c.uses_at(b, q), Chain(steps, 2 * PRE_STEPS + (PRE_STEPS + POST_STEPS) * b.idx)),
                             table(Uses(0, 0), Chain(steps, 0)))


def take_logits(nc, dve, r, logits, chain):
    chain.did(nc.vector.tensor_scalar(r.l[:, :, :], logits, 1.0 / WS, None, ALU.mult))
    chain.wait(dve)


def route_vector(nc, dve, r, chain):
    V = nc.vector
    over = lambda ap: ap.unsqueeze(2).to_broadcast([P, NT, E])

    def did(ins):
        chain.did(ins)
        chain.wait(dve)

    def pick(l, m, oh):
        did(V.tensor_reduce(m, l, AX, ALU.max))
        did(V.tensor_tensor(r.t[:, :, :], l, over(m), ALU.is_equal))
        did(V.tensor_tensor(r.t[:, :, :], r.t[:, :, :], r.desc[:, :, :], ALU.mult))
        did(V.tensor_reduce(r.k[:, :], r.t[:, :, :], AX, ALU.max))
        did(V.tensor_tensor(oh, r.desc[:, :, :], over(r.k[:, :]), ALU.is_equal))

    pick(r.l[:, :, :], r.m1[:, :], r.oh1[:, :, :])
    did(V.scalar_tensor_tensor(out=r.l2[:, :, :], in0=r.oh1[:, :, :], scalar=-BIG, in1=r.l[:, :, :],
                               op0=ALU.mult, op1=ALU.add))
    pick(r.l2[:, :, :], r.m2[:, :], r.oh2[:, :, :])


class Router:
    def __init__(self, nc, ctx, tag):
        sb = lambda name, shape: ctx.enter_context(nc.sbuf_tensor(f"{tag}_{name}", shape, F32))
        self.l, self.l2, self.t, self.oh1, self.oh2, self.desc, self.ex = (
            sb(n, [P, NT, E]) for n in ("l", "l2", "t", "oh1", "oh2", "desc", "ex"))
        self.k, self.m1, self.m2, self.w1, self.w2, self.s = (
            sb(n, [P, NT]) for n in ("k", "m1", "m2", "w1", "w2", "s"))


def layer0_experts(nc, g, w_router, w_gate, w_up, w_down, desc):
    CH = 512
    NC = NB * S0 // CH
    with ExitStack() as ctx:
        sb = lambda name, shape, dt: ctx.enter_context(nc.sbuf_tensor(f"b_{name}", shape, dt))
        sem = lambda name: ctx.enter_context(nc.semaphore(f"b_{name}"))
        ps = lambda name: ctx.enter_context(nc.psum_tensor(f"b_{name}", [P, 512], F32))
        r = Router(nc, ctx, "b")
        coef = sb("coef", [P, NT, E], F32)
        wrs = sb("wrs", [P, KF, E], F32)
        wrh = sb("wrh", [P, KF, E], F16)
        wrl = sb("wrl", [P, KF, E], F16)
        stage = sb("stage", [P, 2 * KF * F0 + 3 * T0], F32)
        GU = KF * F0
        wh = [sb(f"wh{i}", [P, 2 * GU + 3 * T0], F16) for i in range(2)]
        wl = [sb(f"wl{i}", [P, 2 * GU + 3 * T0], F16) for i in range(2)]
        SG = [sb(f"SG{i}", [P, CH], F32) for i in range(2)]
        HF = sb("HF", [P, CH], F32)
        HH = sb("HH", [P, 3, CH], F16)
        HL = sb("HL", [P, 3, CH], F16)
        G = [ps(f"G{i}") for i in range(2)]
        U = [ps(f"U{i}") for i in range(2)]
        O = [ps(f"O{i}") for i in range(4)]
        r_in, st_in = sem("r_in"), sem("st_in")
        st_clear = sem("st_clear")
        w_hi, w_lo = sem("w_hi"), sem("w_lo")
        wr_hi, wr_lo = sem("wr_hi"), sem("wr_lo")
        logits, routed, ex_done = sem("logits"), sem("routed"), sem("ex_done")
        made, silu, mult = sem("made"), sem("silu"), sem("mult")
        hid, down, added = sem("hid"), sem("down"), sem("added")
        step_sem, gate = sem("dve_step"), sem("gate")

        def part(w, which):
            if which < 2:
                return w[:, which * GU:(which + 1) * GU].rearrange("p (k f) -> p k f", k=KF)
            return w[:, 2 * GU:].rearrange("p (k f) -> p k f", k=3)

        def tile_no(e, cc):
            return NC * e + cc

        with nc.Block() as block:
            @block.sync
            def _(sp):
                sp.dma_start(wrs[:, :, :], w_router.rearrange("(k p) e -> p k e", p=P)).then_inc(r_in, 16)
                sp.dma_start(r.desc[:, :, :], desc).then_inc(r_in, 16)
                sp.wait_ge(st_clear, 1)

                def load(e):
                    sp.dma_start(part(stage, 0), w_gate[e].rearrange("(k p) f -> p k f", p=P)).then_inc(st_in, 16)
                    sp.dma_start(part(stage, 1), w_up[e].rearrange("(k p) f -> p k f", p=P)).then_inc(st_in, 16)
                    d = part(stage, 2)
                    sp.dma_start(d[:, 0:2, :], w_down[e][0:2 * P, :].rearrange("(k p) f -> p k f", p=P)).then_inc(st_in, 16)
                    sp.dma_start(d[0:F0 - 2 * P, 2, :], w_down[e][2 * P:F0, :]).then_inc(st_in, 16)

                load(0)
                with sp.Fori(1, E) as e:
                    sp.wait_ge(w_lo, e)
                    load(e)

            @block.tensor
            def _(pe):
                pe.wait_ge(wr_lo, 1)
                for t in range(NT):
                    n = 0
                    for k in range(KF):
                        for xs, ws in ((g.XTh, wrh), (g.XTl, wrh), (g.XTh, wrl)):
                            mm = nc.tensor.matmul(O[0][:, t * E:(t + 1) * E], xs[:, k, t * P:(t + 1) * P], ws[:, k, :],
                                                  start=(n == 0), stop=(n == 3 * KF - 1))
                            n += 1
                mm.then_inc(logits, 1)

                def step(e, q, cc, rr):
                    s = tile_no(e, cc)
                    if rr == 0:
                        pe.wait_ge(w_lo, e + 1)
                    toks = bass.ds(cc * CH, CH)
                    for ft, (f0, m) in enumerate(F0_TILES):
                        j = (rr + ft) % 2
                        pe.wait_ge(mult, 3 * s + ft + 1)
                        for which, bank in ((0, G[j]), (1, U[j])):
                            h, l = part(wh[q], which), part(wl[q], which)
                            n = 0
                            for k in range(KF):
                                for w, xs in ((h, g.XTh), (h, g.XTl), (l, g.XTh)):
                                    mm = nc.tensor.matmul(bank[0:m, :], w[:, k, f0:f0 + m], xs[:, k, toks],
                                                          start=(n == 0), stop=(n == 3 * KF - 1))
                                    n += 1
                        mm.then_inc(made, 1)
                    dh, dl = part(wh[q], 2), part(wl[q], 2)
                    for k, (f0, m) in enumerate(F0_TILES):
                        pe.wait_ge(hid, 3 * s + k + 2)
                        for t in range(4):
                            if k == 0:
                                pe.wait_ge(added, 4 * s + t + 1)
                            for n, (hs, ws) in enumerate(((HH, dh), (HH, dl), (HL, dh))):
                                mm = nc.tensor.matmul(O[t][:, :], hs[0:m, k, t * P:(t + 1) * P], ws[0:m, k, :],
                                                      start=(k == 0 and n == 0), stop=(k == 2 and n == 2))
                            if k == 2:
                                mm.then_inc(down, 1)

                pe.wait_ge(routed, 1)
                with pe.Fori(0, E // 2) as ep:
                    for q in range(2):
                        with pe.Fori(0, NC // 2) as cp:
                            for rr in range(2):
                                step(2 * ep + q, q, 2 * cp + rr, rr)

            def experts(eng, split_one, step):
                def expert(e, q, last):
                    if not last:
                        split_one(e + 1, 1 - q)
                    with eng.Fori(0, NC // 2) as cp:
                        for rr in range(2):
                            step(e, 2 * cp + rr, rr)
                split_one(0, 0)
                with eng.Fori(0, E // 2 - 1) as ep:
                    for q in range(2):
                        expert(2 * ep + q, q, False)
                expert(E - 2, 0, False)
                expert(E - 1, 1, True)

            @block.scalar
            def _(act):
                act.wait_ge(r_in, 32)
                nc.scalar.activation(wrh[:, :, :], wrs[:, :, :], ACT.Copy, scale=WS).then_inc(wr_hi, 1)

                def split_one(e, q):
                    act.wait_ge(st_in, 64 * (e + 1))
                    act.wait_ge(down, 4 * tile_no(e - 1, 0) + 4 if not isinstance(e, int) or e else 4)
                    nc.scalar.activation(wh[q][:, :], stage[:, :], ACT.Copy, scale=WS).then_inc(w_hi, 1)

                def step(e, cc, rr):
                    s = tile_no(e, cc)
                    for ft, (f0, m) in enumerate(F0_TILES):
                        j = (rr + ft) % 2
                        act.wait_ge(mult, 3 * s + ft + 1)
                        act.wait_ge(made, 3 * s + ft + 1)
                        nc.scalar.activation(SG[j][0:m, :], G[j][0:m, :], ACT.Silu, scale=1.0 / WS).then_inc(silu, 1)

                act.wait_ge(routed, 1)
                nc.scalar.activation(r.w2[:, :], r.s[:, :], ACT.Exp).then_inc(ex_done, 1)
                experts(act, split_one, step)

            @block.vector
            def _(dve):
                chain = Chain(step_sem)

                def did(ins):
                    chain.did(ins)
                    chain.wait(dve)

                V = nc.vector
                V.memset(part(stage, 2)[F0 - 2 * P:P, 2, :], 0.0).then_inc(st_clear, 1)
                dve.sem_inc(mult, 2)
                dve.sem_inc(hid, 1)
                dve.sem_inc(down, 4)
                dve.sem_inc(added, 4)
                dve.wait_ge(wr_hi, 1)
                V.scalar_tensor_tensor(out=wrl[:, :, :], in0=wrs[:, :, :], scalar=WS, in1=wrh[:, :, :],
                                       op0=ALU.mult, op1=ALU.subtract).then_inc(wr_lo, 1)
                dve.wait_ge(logits, 1)
                take_logits(nc, dve, r, O[0][:, 0:NT * E].rearrange("p (t e) -> p t e", t=NT), chain)
                route_vector(nc, dve, r, chain)
                did(V.tensor_tensor(r.s[:, :], r.m2[:, :], r.m1[:, :], ALU.subtract))
                dve.sem_inc(routed, 1)
                dve.wait_ge(ex_done, 1)
                did(V.tensor_scalar(r.w1[:, :], r.w2[:, :], 1.0, None, ALU.add))
                did(V.reciprocal(r.w1[:, :], r.w1[:, :]))
                did(V.tensor_tensor(r.w2[:, :], r.w2[:, :], r.w1[:, :], ALU.mult))
                over = lambda ap: ap.unsqueeze(2).to_broadcast([P, NT, E])
                did(V.tensor_tensor(r.t[:, :, :], r.oh1[:, :, :], over(r.w1[:, :]), ALU.mult))
                did(V.tensor_tensor(r.l2[:, :, :], r.oh2[:, :, :], over(r.w2[:, :]), ALU.mult))
                did(V.tensor_tensor(r.t[:, :, :], r.t[:, :, :], r.l2[:, :, :], ALU.add))
                did(V.tensor_scalar(coef[:, :, :], r.t[:, :, :], 1.0 / WS, None, ALU.mult))

                def split_one(e, q):
                    dve.wait_ge(w_hi, e + 1)
                    V.scalar_tensor_tensor(out=wl[q][:, :], in0=stage[:, :], scalar=WS, in1=wh[q][:, :],
                                           op0=ALU.mult, op1=ALU.subtract).then_inc(w_lo, 1)

                base = chain.n

                def step(e, cc, rr):
                    s = tile_no(e, cc)
                    for ft, (f0, m) in enumerate(F0_TILES):
                        j, i = (rr + ft) % 2, 3 * s + ft
                        dve.wait_ge(silu, i + 1)
                        dve.wait_ge(hid, i + 1)
                        V.scalar_tensor_tensor(out=HF[0:m, :], in0=U[j][0:m, :], scalar=1.0 / WS, in1=SG[j][0:m, :],
                                               op0=ALU.mult, op1=ALU.mult).then_inc(mult, 1)
                        dve.wait_ge(mult, i + 3)
                        dve.wait_ge(down, 4 * s + 4)
                        V.tensor_copy(HH[0:m, ft, :], HF[0:m, :]).then_inc(step_sem, 1)
                        dve.wait_ge(step_sem, base + i + 1)
                        V.tensor_tensor(HL[0:m, ft, :], HF[0:m, :], HH[0:m, ft, :], ALU.subtract).then_inc(hid, 1)
                    for t in range(4):
                        dve.wait_ge(down, 4 * s + t + 5)
                        acc = g.x1[:, 4 * cc + t, :]
                        V.scalar_tensor_tensor(out=acc, in0=O[t][:, :], scalar=coef[:, 4 * cc + t, bass.ds(e, 1)],
                                               in1=acc, op0=ALU.mult, op1=ALU.add).then_inc(added, 1)

                experts(dve, split_one, step)


def layer1_attention(nc, g, cond, w_emb, b_emb, g_norm, w_qkv, g_q, g_k, w_out, sel):
    c = Core(heads=16, n=S0, n_pre=10, n_v=2, v_opening=1, mask_row=False, lag=8, dt=F16)
    EPS = 1e-6
    D = T0 // c.heads
    with ExitStack() as ctx:
        a = Attention(nc, ctx, "c", c, g.ident)
        sb = lambda name, shape, dt: ctx.enter_context(nc.sbuf_tensor(f"c_{name}", shape, dt))
        sem = lambda name: ctx.enter_context(nc.semaphore(f"c_{name}"))
        wqh = sb("wqh", [P, KF, 3 * T0], F16)
        wql = sb("wql", [P, KF, 3 * T0], F16)
        woh = sb("woh", [P, KF, T0], F16)
        wol = sb("wol", [P, KF, T0], F16)
        gcol = sb("gcol", [P, 2], F32)
        gs = sb("gs", [P, KF, NB], F32)
        sh = sb("sh", [P, KF, NB], F32)
        rstd = sb("rstd", [P, NT], F32)
        XX = sb("XX", [P, 4 * T0], F32)
        XS = XX[:, 0:2 * T0].rearrange("p (t f) -> p t f", t=2)
        XN = XX[:, 2 * T0:4 * T0].rearrange("p (k s) -> p k s", k=KF)
        SQ = XX[:, :].rearrange("p (t w f) -> p t w f", t=2, w=2)
        XNh = [sb(f"XNh{i}", [P, KF, S0], F16) for i in range(2)]
        XNl = [sb(f"XNl{i}", [P, KF, S0], F16) for i in range(2)]
        QK = sb("QK", [P, 2, 2, T0], F32)
        ssq = sb("ssq", [P, 2 * 2 * 16], F32)
        H = [sb(f"H{i}", [P, KF, S0], F16) for i in range(2)]
        L = [sb(f"L{i}", [P, KF, S0], F16) for i in range(2)]
        CH = sb("CH", [P, KF, S0], F16)
        CL = sb("CL", [P, KF, S0], F16)
        p_in, p_act, p_dve, p_pe = sem("p_in"), sem("p_act"), sem("p_dve"), sem("p_pe")
        q_in = [sem(f"q_in{i}") for i in range(6)]
        p_sq = sem("p_sq")
        begun, xn_hi, qk_hi = sem("begun"), sem("xn_hi"), sem("qk_hi")
        xs_done, xn_done, qk_out, sq_done, var_done, std_done, qn_done = (
            sem(n) for n in ("xs_done", "xn_done", "qk_out", "sq_done", "var_done", "std_done", "qn_done"))

        with ExitStack() as setup:
            tmp = lambda name, shape: setup.enter_context(nc.sbuf_tensor(f"cs_{name}", shape, F32))
            ws = [QK[:, :, :, :].rearrange("p a b f -> p (a b) f"), XX[:, :].rearrange("p (k f) -> p k f", k=KF)]
            ws += [a.V[i][:, :, :, :].rearrange("p t h d -> p (t h d)").rearrange("p (k f) -> p k f", k=KF) for i in range(2)]
            ws += ws[0:2]
            ones_set = setup.enter_context(nc.semaphore("c_ones_set"))
            cn = a.CS[0:NB, 0:2, :].rearrange("b a f -> b (a f)")
            condT = tmp("condT", [P, KF, NB])
            vrow = a.CS[0:3 * KF, 2, 0:P]
            vec = tmp("vec", [P, 3, KF])
            with nc.Block() as block:
                @block.gpsimd
                def _(pool):
                    for k, buf in enumerate((a.B[0][96:97, :, :], a.B[1][96:97, :, :], a.V[0][:, :, :, :], a.V[1][:, :, :, :])):
                        if k >= 2:
                            pool.wait_ge(p_dve, k + 1)
                        nc.gpsimd.memset(buf, 1.0).then_inc(ones_set, 1)
                        pool.wait_ge(ones_set, k + 1)

                @block.sync
                def _(sp):
                    sp.dma_start(cn, cond).then_inc(p_in, 16)
                    sp.dma_start(vrow[0:2 * KF, :], b_emb.rearrange("(k p) -> k p", p=P)).then_inc(p_in, 16)
                    sp.dma_start(vrow[2 * KF:3 * KF, :], g_norm.rearrange("(k p) -> k p", p=P)).then_inc(p_in, 16)
                    for j in range(4):
                        for i, v in enumerate((g_q, g_k)):
                            sp.dma_start(gcol[32 * j:32 * j + 32, i:i + 1], v.rearrange("(p a) -> p a", a=1)).then_inc(p_in, 16)
                    sp.dma_start(a.SEL[:, :, :], sel).then_inc(p_in, 16)
                    for i in range(6):
                        src = (w_qkv[:, i * T0:(i + 1) * T0] if i < 3 else w_out if i == 3
                               else w_emb[:, (i - 4) * T0:(i - 3) * T0])
                        if i >= 4:
                            sp.wait_ge(p_dve, i - 3)
                        sp.dma_start(ws[i], src.rearrange("(k p) f -> p k f", p=P)).then_inc(q_in[i], 16)

                @block.scalar
                def _(act):
                    for t in range(NT):
                        if t >= 4:
                            act.wait_ge(p_sq, t - 3)
                        nc.scalar.activation(a.EX[t % 4][:, :], g.x1[:, t, :], ACT.Square,
                                             accum_out=rstd[:, t:t + 1]).then_inc(p_sq, 1)
                    for i in range(4):
                        act.wait_ge(q_in[i], 16)
                        dst = wqh[:, :, i * T0:(i + 1) * T0] if i < 3 else woh[:, :, :]
                        nc.scalar.activation(dst, ws[i], ACT.Copy, scale=WS).then_inc(p_act, 1)
                    act.wait_ge(p_dve, 11)
                    nc.scalar.activation(rstd[:, :], rstd[:, :], ACT.Sqrt).then_inc(p_act, 1)

                @block.tensor
                def _(pe):
                    pe.wait_ge(p_in, 16 * 12)
                    for k in range(KF):
                        mm = nc.tensor.transpose(a.pp[0][:, k * NB:(k + 1) * NB], cn[:, k * P:(k + 1) * P], g.ident[0:NB, 0:NB])
                    mm = nc.tensor.transpose(a.pp[0][:, KF * NB:KF * NB + 3 * KF], vrow, g.ident[0:3 * KF, 0:3 * KF])
                    mm.then_inc(p_pe, 1)
                    pe.wait_ge(p_dve, 5)
                    for i in range(2):
                        pe.wait_ge(q_in[4 + i], 16)
                        for o in range(KF):
                            for k in range(KF):
                                mm = nc.tensor.matmul(a.pp[1][:, (i * KF + o) * NB:(i * KF + o + 1) * NB],
                                                      ws[4 + i][:, k, o * P:(o + 1) * P], condT[:, k, :],
                                                      start=(k == 0), stop=(k == KF - 1))
                        mm.then_inc(p_pe, 1)

                @block.vector
                def _(dve):
                    V = nc.vector
                    for i in range(4):
                        dve.wait_ge(p_act, i + 1)
                        hi, dst = ((wqh[:, :, i * T0:(i + 1) * T0], wql[:, :, i * T0:(i + 1) * T0]) if i < 3
                                   else (woh[:, :, :], wol[:, :, :]))
                        V.scalar_tensor_tensor(out=dst, in0=ws[i], scalar=WS, in1=hi,
                                               op0=ALU.mult, op1=ALU.subtract).then_inc(p_dve, 1)
                    dve.wait_ge(p_pe, 1)
                    V.tensor_copy(condT[:, :, :], a.pp[0][:, 0:KF * NB].rearrange("p (k b) -> p k b", k=KF)).then_inc(p_dve, 1)
                    V.tensor_copy(vec[:, :, :], a.pp[0][:, KF * NB:KF * NB + 3 * KF].rearrange("p (s k) -> p s k", s=3)).then_inc(p_dve, 1)
                    dve.wait_ge(p_dve, 6)
                    dve.wait_ge(p_pe, 3)
                    ss = a.pp[1][:, 0:2 * KF * NB].rearrange("p (s k b) -> p s k b", s=2, k=KF)
                    over = lambda ap: ap.unsqueeze(2).to_broadcast([P, KF, NB])
                    V.tensor_tensor(sh[:, :, :], ss[:, 1, :, :], over(vec[:, 1, :]), ALU.add).then_inc(p_dve, 1)
                    V.tensor_tensor(gs[:, :, :], ss[:, 0, :, :], over(vec[:, 0, :]), ALU.add).then_inc(p_dve, 1)
                    dve.wait_ge(p_dve, 8)
                    V.scalar_tensor_tensor(out=gs[:, :, :], in0=gs[:, :, :], scalar=1.0, in1=over(vec[:, 2, :]),
                                           op0=ALU.add, op1=ALU.mult).then_inc(p_dve, 1)
                    dve.wait_ge(p_sq, NT)
                    V.tensor_scalar(rstd[:, :], rstd[:, :], 1.0 / T0, EPS, ALU.mult, ALU.add).then_inc(p_dve, 1)
                    dve.wait_ge(p_dve, 10)
                    V.reciprocal(rstd[:, :], rstd[:, :]).then_inc(p_dve, 1)
                    V.tensor_scalar(gcol[:, 0:1], gcol[:, 0:1], float(D ** -0.5), None, ALU.mult).then_inc(p_dve, 1)
                    dve.wait_ge(p_dve, 12)
                    dve.wait_ge(ones_set, 4)

        pre = ("xs", "xt0", "xt1", "q0", "k0", "q1", "k1", "square0", "sum0", "square1", "sum1", "norm", "root", "scale", "qk")
        plan = c.plan(7, {1: ("recip",), 2: ("spread",), 6: ("out",), 7: ("xs",), 8: ("xt0", "xt1"), 9: ("q0",), 10: ("k0",),
                          11: ("q1", "square0"), 12: ("k1", "sum0"), 13: ("square1",), 14: ("sum1", "norm"), 15: ("root",)},
                      ("shift", "scale", "v0", "qk", "v1"))

        with nc.Block() as block:
            @block.gpsimd
            def _(pool):
                rows = lambda n: a.assemble(pool, n, a.B, a.b_in, (H[1], H[1], L[1]))
                rows(Batch(0, 0))
                rows(Batch(0, 1))
                with pool.Fori(0, NB // 2 - 1) as i:
                    for q in range(2):
                        rows(Batch(i, q + 2))

            @block.sync
            def _(sp):
                rows = lambda n: a.assemble(sp, n, a.A, a.a_in, (H[0], L[0], H[0]))
                rows(Batch(0, 0))
                rows(Batch(0, 1))
                with sp.Fori(0, NB // 2 - 1) as i:
                    for q in range(2):
                        a.sp_context(sp, Batch(i, q))
                        rows(Batch(i, q + 2))
                a.sp_context(sp, Batch(NB // 2 - 1, 0))
                a.sp_context(sp, Batch(NB // 2 - 1, 1))

            @block.tensor
            def _(pe):
                def x_turned(n, uses, u):
                    pe.wait_ge(xs_done, n.idx + 1)
                    bank = a.pe_take(pe, uses)
                    for kk in range(2):
                        for t in range(2):
                            mm = nc.tensor.transpose(bank[:, kk * S0 + t * P:kk * S0 + (t + 1) * P],
                                                     XS[:, t, (2 * u + kk) * P:(2 * u + kk + 1) * P], g.ident[:, :])
                    mm.then_inc(a.proj_made, 1)

                def project(n, uses, t, j):
                    pe.wait_ge(xn_done, 2 * (n.idx + 1))
                    bank = a.pe_take(pe, uses)
                    for k in range(KF):
                        for m, (xs, ws) in enumerate(((XNh[n.par], wqh), (XNh[n.par], wql), (XNl[n.par], wqh))):
                            mm = nc.tensor.matmul(bank[:, :], xs[:, k, t * P:(t + 1) * P],
                                                  ws[:, k, j * T0:(j + 1) * T0],
                                                  start=(k == 0 and m == 0), stop=(k == KF - 1 and m == 2))
                    mm.then_inc(a.proj_made, 1)

                def pre_qk(n, uses):
                    pe.wait_ge(qn_done, n.idx + 1)
                    for w in range(2):
                        for u in range(2):
                            bank = a.pe_take(pe, uses)
                            for kk in range(2):
                                for t in range(2):
                                    mm = nc.tensor.transpose(bank[:, kk * S0 + t * P:kk * S0 + (t + 1) * P],
                                                             QK[:, t, w, (2 * u + kk) * P:(2 * u + kk + 1) * P], g.ident[:, :])
                            mm.then_inc(a.proj_made, 1)

                def out(n, uses):
                    pe.wait_ge(a.ctx_norm, 2 * (n.idx + 1))
                    for u in range(2):
                        bank = a.pe_take(pe, uses)
                        for dd in range(2):
                            d = 2 * u + dd
                            for k in range(KF):
                                for m, (ws, xs) in enumerate(((woh, CH), (woh, CL), (wol, CH))):
                                    mm = nc.tensor.matmul(bank[:, dd * S0:(dd + 1) * S0], ws[:, k, d * P:(d + 1) * P],
                                                          xs[:, k, :], start=(k == 0 and m == 0),
                                                          stop=(k == KF - 1 and m == 2))
                        mm.then_inc(a.proj_made, 1)

                def table(uses):
                    steps = {"first": lambda n: a.pe_first(pe, n), "slot": lambda n, s: a.pe_slot(pe, n, s),
                             "nat": lambda n, s: a.pe_nat(pe, n, s), "shift": lambda n: a.pe_shift(pe, n, uses),
                             "xt0": lambda n: x_turned(n, uses, 0), "xt1": lambda n: x_turned(n, uses, 1),
                             "qk": lambda n: pre_qk(n, uses), 
                             "spread": lambda n: a.pe_spread(pe, n, uses), "out": lambda n: out(n, uses)}
                    for t in range(2):
                        for j, name in enumerate("qkv"):
                            steps[f"{name}{t}"] = lambda n, t=t, j=j: project(n, uses, t, j)
                    return steps

                batches(pe, c, plan, pre, ("v0", "v1"), lambda b, q: table(c.uses_at(b, q)), table(Uses(0, 0)))

            @block.scalar
            def _(act):
                def square(n, t):
                    act.wait_ge(qk_out, 4 * n.idx + 2 * (t + 1))
                    nc.scalar.activation(SQ[:, t, :, :], QK[:, t, :, :], ACT.Square).then_inc(sq_done, 1)

                def root(n):
                    act.wait_ge(var_done, n.idx + 1)
                    nc.scalar.activation(ssq[:, :], ssq[:, :], ACT.Sqrt).then_inc(std_done, 1)

                def modulate(n, uses, u):
                    bank = a.taken(act, uses)
                    act.sem_inc(begun, 1)
                    for dst in (XN, XNh[n.par]):
                        for k in (2 * u, 2 * u + 1):
                            ins = nc.scalar.activation(dst[:, k, :], bank[:, (k - 2 * u) * S0:(k - 2 * u + 1) * S0],
                                                       ACT.Identity, scale=gs[:, k, bass.ds(n.idx, 1)],
                                                       bias=sh[:, k, bass.ds(n.idx, 1)])
                    ins.then_inc(xn_hi, 1)

                def turned_qk(n, uses):
                    for w in range(2):
                        for u in range(2):
                            bank = a.taken(act, uses)
                            if w == 0 and u == 0 and not n.first:
                                act.wait_ge(a.a_in, 16 * a.AB_DMAS * n.idx)
                                act.wait_ge(a.b_in, 16 * a.AB_DMAS * n.idx)
                            nc.scalar.activation(H[w][:, 2 * u:2 * u + 2, :], bank[:, :].rearrange("p (k s) -> p k s", k=2),
                                                 ACT.Copy, scale=gcol[:, w:w + 1]).then_inc(qk_hi, 1)

                def shift(n, uses):
                    a.act_shift(act, n)
                    uses.take()

                def table(uses):
                    steps = {"slot": lambda n, s: a.act_slot(act, n, s), "shift": lambda n: shift(n, uses),
                             "xt0": lambda n: modulate(n, uses, 0), "xt1": lambda n: modulate(n, uses, 1),
                             "qk": lambda n: turned_qk(n, uses),
                             "square0": lambda n: square(n, 0), "square1": lambda n: square(n, 1), "root": root}
                    for name, k in {"q0": 1, "k0": 1, "q1": 1, "k1": 1, "v0": 1, "v1": 1, "spread": 2, "out": 2}.items():
                        steps[name] = lambda n, k=k: [uses.take() for _ in range(k)]
                    return steps

                batches(act, c, plan, pre, ("v0", "v1"), lambda b, q: table(c.uses_at(b, q)), table(Uses(0, 0)))

            @block.vector
            def _(dve):
                V = nc.vector
                a.prime(dve)

                def xs(n, chain):
                    for t in range(2):
                        ins = V.tensor_scalar(XS[:, t, :], g.x1[:, 2 * n.idx + t, :],
                                              rstd[:, bass.ds(2 * n.idx + t, 1)], None, ALU.mult)
                        if t == 0:
                            chain.did(ins)
                    chain.wait(dve)
                    ins.then_inc(xs_done, 1)

                def modulate(n, uses, u):
                    uses.take()
                    dve.wait_ge(xn_hi, 2 * n.idx + u + 1)
                    dve.sem_inc(a.proj_out, 1)
                    ks = slice(2 * u, 2 * u + 2)
                    V.tensor_tensor(XNl[n.par][:, ks, :], XN[:, ks, :], XNh[n.par][:, ks, :], ALU.subtract).then_inc(xn_done, 1)

                def take_qk(n, uses, t, w):
                    bank = a.taken(dve, uses)
                    V.tensor_scalar(QK[:, t, w, :], bank[:, :], 1.0 / WS, None, ALU.mult).then_inc(qk_out, 1)
                    dve.wait_ge(qk_out, 4 * n.idx + 2 * t + w + 1)
                    dve.sem_inc(a.proj_out, 1)

                def take_v(n, uses, t):
                    bank = a.taken(dve, uses)
                    V.tensor_scalar(a.V[n.par][:, t, :, 0:32], bank[:, :].rearrange("p (h d) -> p h d", h=c.heads),
                                    1.0 / WS, None, ALU.mult).then_inc(a.proj_out, 1)
                    if t == 1:
                        dve.wait_ge(a.proj_out, uses.base + uses.k + 2)
                        dve.sem_inc(a.v_ready, 1)

                heads = lambda ap: ap.rearrange("p t w (h d) -> p (t w h) d", d=D)

                def sums(n, chain, t):
                    dve.wait_ge(sq_done, 2 * n.idx + t + 1)
                    chain.did(V.tensor_reduce(ssq[:, t * 2 * c.heads:(t + 1) * 2 * c.heads],
                                              heads(SQ[:, t:t + 1, :, :]), AX, ALU.add))

                def norm(n, chain):
                    chain.wait(dve)
                    chain.did(V.tensor_scalar(ssq[:, :], ssq[:, :], 1.0 / D, EPS, ALU.mult, ALU.add))
                    chain.wait(dve)
                    V.reciprocal(ssq[:, :], ssq[:, :]).then_inc(var_done, 1)

                def scale(n):
                    dve.wait_ge(std_done, n.idx + 1)
                    qk = heads(QK[:, :, :, :])
                    V.tensor_tensor(qk, qk, ssq[:, :].unsqueeze(2).to_broadcast([P, 64, D]), ALU.mult).then_inc(qn_done, 1)

                def pre_qk(n, uses, chain):
                    for w in range(2):
                        for u in range(2):
                            bank = a.taken(dve, uses)
                            dve.wait_ge(qk_hi, 4 * n.idx + 2 * w + u + 1)
                            ks = slice(2 * u, 2 * u + 2)
                            chain.did(V.scalar_tensor_tensor(out=L[w][:, ks, :], in0=bank[:, :].rearrange("p (k s) -> p k s", k=2),
                                                             scalar=gcol[:, w:w + 1], in1=H[w][:, ks, :],
                                                             op0=ALU.mult, op1=ALU.subtract))
                            chain.wait(dve)
                            dve.sem_inc(a.proj_out, 1)
                    dve.sem_inc(a.split_done, 1)

                def spread(n, uses, chain):
                    for u in range(2):
                        bank = a.taken(dve, uses)
                        ks = slice(2 * u, 2 * u + 2)
                        chain.did(V.tensor_tensor(a.CT[:, ks, :], a.CT[:, ks, :],
                                                  bank[:, :].rearrange("p (k s) -> p k s", k=2), ALU.mult))
                        chain.wait(dve)
                        dve.sem_inc(a.proj_out, 1)
                        chain.did(V.tensor_copy(CH[:, ks, :], a.CT[:, ks, :]))
                        chain.wait(dve)
                        V.tensor_tensor(CL[:, ks, :], a.CT[:, ks, :], CH[:, ks, :], ALU.subtract).then_inc(a.ctx_norm, 1)

                def out(n, uses, chain):
                    for u in range(2):
                        bank = a.taken(dve, uses)
                        ks = slice(2 * u, 2 * u + 2)
                        ps = bank[:, :].rearrange("p (k s) -> p k s", k=2)
                        chain.did(V.scalar_tensor_tensor(out=a.CT[:, ks, :], in0=ps, scalar=1.0 / WS, in1=a.CT[:, ks, :],
                                                         op0=ALU.mult, op1=ALU.add))
                        chain.wait(dve)
                        dve.sem_inc(a.proj_out, 1)
                        hi = g.XTh[:, ks, bass.ds(n.idx * S0, S0)]
                        lo = g.XTl[:, ks, bass.ds(n.idx * S0, S0)]
                        chain.did(V.tensor_copy(hi, a.CT[:, ks, :]))
                        chain.wait(dve)
                        chain.did(V.tensor_tensor(lo, a.CT[:, ks, :], hi, ALU.subtract))
                    chain.wait(dve)
                    dve.sem_inc(a.post_done, 1)

                PRE, POST = 1 + 3 + 4, 4 + 6

                def table(uses, chain):
                    steps = {"nat": lambda n, s: a.dve_max(dve, n, s), "shift": lambda n: a.dve_shift(dve, n, uses),
                             "xs": lambda n: xs(n, chain), "xt0": lambda n: modulate(n, uses, 0),
                             "xt1": lambda n: modulate(n, uses, 1), "norm": lambda n: norm(n, chain),
                             "scale": scale, "qk": lambda n: pre_qk(n, uses, chain), 
                             "sum0": lambda n: sums(n, chain, 0), "sum1": lambda n: sums(n, chain, 1),
                             "recip": lambda n: a.dve_recip(dve, n), "spread": lambda n: spread(n, uses, chain),
                             "out": lambda n: out(n, uses, chain)}
                    for t in range(2):
                        for j, name in enumerate("qk"):
                            steps[f"{name}{t}"] = lambda n, t=t, j=j: take_qk(n, uses, t, j)
                        steps[f"v{t}"] = lambda n, t=t: take_v(n, uses, t)
                    return steps

                batches(dve, c, plan, pre, ("v0", "v1"),
                        lambda b, q: table(c.uses_at(b, q), Chain(a.dve_step, 2 * PRE + (PRE + POST) * b.idx)),
                        table(Uses(0, 0), Chain(a.dve_step, 0)))


def layer1_experts(nc, g, Wg, Wu, Wd, Wr, Ag, Bg, Au, Bu, Ad, Bd, desc, out):
    LORA = 2.0
    CH = S0
    ER = E * R
    ITEMS = [(kind, f) for i in range(FT + 2) for kind, f in ((0, i), (1, i - 1), (2, i - 2)) if 0 <= f < FT]
    NI = len(ITEMS)
    NUM = {it: k for k, it in enumerate(ITEMS)}
    with ExitStack() as ctx:
        sb = lambda name, shape, dt: ctx.enter_context(nc.sbuf_tensor(f"d_{name}", shape, dt))
        sem = lambda name: ctx.enter_context(nc.semaphore(f"d_{name}"))
        bank = [ctx.enter_context(nc.psum_tensor(f"d_bank{i}", [P, 512], F32)) for i in range(8)]
        GU, O, Z = bank[0:4], bank[4:6], bank[6:8]
        two = lambda name, shape: (sb(name + "h", shape, F16), sb(name + "l", shape, F16))
        wg, wu, wd = two("wg", [P, KF, DFF]), two("wu", [P, KF, DFF]), two("wd", [P, FT, T0])
        bgu = two("bgu", [ER, 2, DFF])
        agu = two("agu", [P, 2, KF, ER])
        ad, bd = two("ad", [P, FT, ER]), two("bd", [ER, T0])
        wr = two("wr", [P, KF, E])
        r = Router(nc, ctx, "d")
        kinds = sb("kinds", [P, NT, 4, E], F32)
        EX = sb("EX", [P, 2, 4, E, R], F32)
        SG = [sb(f"SG{i}", [P, CH], F32) for i in range(3)]
        HF = sb("HF", [P, CH], F32)
        HS = [[two(f"H{kind}{i}_", [P, CH]) for i in range(2)] for kind in range(3)]
        al = two("al", [ER, 2, CH])
        M = [two(f"M{i}", [ER, 2, CH]) for i in range(2)]
        MK = sb("MK", [ER, 2, CH], F16)
        MW = sb("MW", [ER, 2, CH], F32)
        ZZ = sb("ZZ", [ER, 2, CH], F32)
        zz = two("zz", [ER, CH])
        Y = [sb(f"Y{i}", [P, T0], F32) for i in range(2)]
        step_sem = sem("dve_step")

        with ExitStack() as setup:
            tmp = lambda name, shape: setup.enter_context(nc.sbuf_tensor(f"ds_{name}", shape, F32))
            sg, su = ([tmp(f"{n}{i}", [P, T0]) for i in range(2)] for n in ("sg", "su"))
            sd = [tmp(f"sd{i}", [P, KF, P]) for i in range(2)]
            sbg, sbu = ([tmp(f"{n}{i}", [P, E, R]) for i in range(2)] for n in ("sbg", "sbu"))
            sa = [tmp(f"sa{i}", [ER, P]) for i in range(2)]
            first_in = sem("first_in")
            t_in = [sem("t_in0"), sem("t_in1")]
            turned, hi_done, lo_done = sem("turned"), sem("hi_done"), sem("lo_done")
            first_hi, first_lo = sem("first_hi"), sem("first_lo")
            logits, routed, exped = sem("logits"), sem("routed"), sem("exped")
            fa, fu = Y[0], Y[1]
            fb = ZZ[:, :, :].rearrange("p a c -> p (a c)").rearrange("p (t e r) -> p t e r", t=KF, e=E)
            fr = EX[0:E, 0, :, :, :].rearrange("p k e r -> p (k e r)")

            def each_tile(eng, step):
                with eng.Fori(0, FT // 2) as i:
                    for q in range(2):
                        step(Batch(i, q))
                step(Batch(FT // 2, 0))

            def outputs(n):
                b = bank[4 * n.par:4 * n.par + 4]
                cols = bass.ds(n.idx * P, P)
                v = lambda x: x[:, :].rearrange("p (k c) -> p k c", k=KF)
                return [(v(b[0]), wg, lambda w: w[:, :, cols], WS), (v(b[1]), wu, lambda w: w[:, :, cols], WS),
                        (b[2][:, :], wd, lambda w: w[:, n.idx, :], WS),
                        (b[3][:, 0:2 * P].rearrange("p (w c) -> p w c", w=2), bgu, lambda w: w[:, :, cols], LORA * WS),
                        (b[3][:, 2 * P:3 * P], ad, lambda w: w[:, n.idx, :], WS)]

            v4 = lambda x: x[:, :].rearrange("p (k c) -> p k c", k=KF)
            firsts = [(v4(bank[0]), agu, lambda w: w[:, 0, :, :], WS), (v4(bank[1]), agu, lambda w: w[:, 1, :, :], WS),
                      (bank[2][:, :], bd, lambda w: w[:, :], LORA * WS),
                      (bank[3][:, 0:KF * E].rearrange("p (k e) -> p k e", k=KF), wr, lambda w: w[:, :, :], WS)]

            with nc.Block() as block:
                @block.sync
                def _(sp):
                    sp.dma_start(fa[:, :], Ag.rearrange("e r f -> (e r) f")).then_inc(first_in, 16)
                    sp.dma_start(fu[:, :], Au.rearrange("e r f -> (e r) f")).then_inc(first_in, 16)
                    sp.dma_start(fr, Wr).then_inc(first_in, 16)
                    for k in range(KF):
                        sp.dma_start(fb[:, k, :, :], Bd[:, k * P:(k + 1) * P, :].rearrange("e p r -> p e r")).then_inc(first_in, 16)
                    sp.dma_start(r.desc[:, :, :], desc).then_inc(first_in, 16)

                    def load(n):
                        rows = bass.ds(n.idx * P, P)
                        if not (isinstance(n.idx, int) and n.idx < 2):
                            sp.wait_ge(turned, n.idx - 1 + 1)
                        sp.dma_start(sg[n.par][:, :], Wg[rows, :]).then_inc(t_in[n.par], 16)
                        sp.dma_start(su[n.par][:, :], Wu[rows, :]).then_inc(t_in[n.par], 16)
                        sp.dma_start(sd[n.par][:, :, :], Wd[:, rows].rearrange("(k p) c -> p k c", p=P)).then_inc(t_in[n.par], 16)
                        sp.dma_start(sbg[n.par][:, :, :], Bg[:, rows, :].rearrange("e p r -> p e r")).then_inc(t_in[n.par], 16)
                        sp.dma_start(sbu[n.par][:, :, :], Bu[:, rows, :].rearrange("e p r -> p e r")).then_inc(t_in[n.par], 16)
                        sp.dma_start(sa[n.par][:, :], Ad.rearrange("e r c -> (e r) c")[:, rows]).then_inc(t_in[n.par], 16)

                    load(Batch(0, 0))
                    load(Batch(0, 1))
                    with sp.Fori(1, FT // 2) as i:
                        for q in range(2):
                            load(Batch(i, q))
                    load(Batch(FT // 2, 0))

                @block.tensor
                def _(pe):
                    T = nc.tensor.transpose
                    pe.wait_ge(first_in, 16 * 8)
                    for k in range(KF):
                        T(bank[0][:, k * P:(k + 1) * P], fa[:, k * P:(k + 1) * P], g.ident[:, :])
                        T(bank[1][:, k * P:(k + 1) * P], fu[:, k * P:(k + 1) * P], g.ident[:, :])
                        T(bank[2][:, k * P:(k + 1) * P], fb[:, k, :, :].rearrange("p e r -> p (e r)"), g.ident[:, :])
                        mm = T(bank[3][:, k * E:(k + 1) * E], fr[:, k * P:(k + 1) * P], g.ident[0:E, 0:E])
                    mm.then_inc(turned, 1)
                    pe.wait_ge(first_lo, 1)
                    for t in range(NT):
                        n = 0
                        for k in range(KF):
                            for xs, ws in ((g.XTh, wr[0]), (g.XTl, wr[0]), (g.XTh, wr[1])):
                                mm = nc.tensor.matmul(bank[7][:, t * E:(t + 1) * E], xs[:, k, t * P:(t + 1) * P], ws[:, k, :],
                                                      start=(n == 0), stop=(n == 3 * KF - 1))
                                n += 1
                    mm.then_inc(logits, 1)

                    def step(n):
                        pe.wait_ge(t_in[n.par], 96 * (n.half + 1))
                        pe.wait_ge(lo_done, n.idx + 1)
                        b = bank[4 * n.par:4 * n.par + 4]
                        for k in range(KF):
                            ks = slice(k * P, (k + 1) * P)
                            T(b[0][:, ks], sg[n.par][:, ks], g.ident[:, :])
                            T(b[1][:, ks], su[n.par][:, ks], g.ident[:, :])
                            T(b[2][:, ks], sd[n.par][:, k, :], g.ident[:, :])
                        T(b[3][:, 0:P], sbg[n.par][:, :, :].rearrange("p e r -> p (e r)"), g.ident[:, :])
                        T(b[3][:, P:2 * P], sbu[n.par][:, :, :].rearrange("p e r -> p (e r)"), g.ident[:, :])
                        T(b[3][:, 2 * P:3 * P], sa[n.par][:, :], g.ident[:, :]).then_inc(turned, 1)

                    each_tile(pe, step)

                @block.scalar
                def _(act):
                    act.wait_ge(turned, 1)
                    for src, w, dst, scale in firsts:
                        ins = nc.scalar.activation(dst(w[0]), src, ACT.Copy, scale=scale)
                    ins.then_inc(first_hi, 1)

                    def step(n):
                        act.wait_ge(turned, n.idx + 2)
                        for src, w, dst, scale in outputs(n):
                            ins = nc.scalar.activation(dst(w[0]), src, ACT.Copy, scale=scale)
                        ins.then_inc(hi_done, 1)

                    each_tile(act, step)
                    act.wait_ge(routed, 1)
                    nc.scalar.activation(r.ex[:, :, :], r.t[:, :, :], ACT.Exp)
                    nc.scalar.activation(r.w2[:, :], r.s[:, :], ACT.Exp).then_inc(exped, 1)

                @block.vector
                def _(dve):
                    V = nc.vector
                    chain = Chain(step_sem)

                    def did(ins):
                        chain.did(ins)
                        chain.wait(dve)

                    dve.sem_inc(lo_done, 1)
                    dve.wait_ge(first_hi, 1)
                    for src, w, dst, scale in firsts:
                        ins = V.scalar_tensor_tensor(out=dst(w[1]), in0=src, scalar=scale, in1=dst(w[0]),
                                                     op0=ALU.mult, op1=ALU.subtract)
                    ins.then_inc(first_lo, 1)
                    dve.wait_ge(logits, 1)
                    take_logits(nc, dve, r, bank[7][:, 0:NT * E].rearrange("p (t e) -> p t e", t=NT), chain)
                    dve.sem_inc(lo_done, 1)
                    over = lambda ap: ap.unsqueeze(2).to_broadcast([P, NT, E])
                    route_vector(nc, dve, r, chain)
                    did(V.tensor_tensor(r.s[:, :], r.m2[:, :], r.m1[:, :], ALU.subtract))
                    did(V.tensor_tensor(r.t[:, :, :], r.l[:, :, :], over(r.m1[:, :]), ALU.subtract))
                    dve.sem_inc(routed, 1)

                    def step(n):
                        dve.wait_ge(hi_done, n.idx + 1)
                        for src, w, dst, scale in outputs(n):
                            ins = V.scalar_tensor_tensor(out=dst(w[1]), in0=src, scalar=scale, in1=dst(w[0]),
                                                         op0=ALU.mult, op1=ALU.subtract)
                        ins.then_inc(lo_done, 1)

                    each_tile(dve, step)
                    dve.wait_ge(exped, 1)
                    did(V.tensor_reduce(r.w1[:, :], r.ex[:, :, :], AX, ALU.add))
                    did(V.reciprocal(r.w1[:, :], r.w1[:, :]))
                    did(V.tensor_scalar(r.w1[:, :], r.w1[:, :], 1.0 / WS, None, ALU.mult))
                    did(V.tensor_tensor(r.w2[:, :], r.w2[:, :], r.w1[:, :], ALU.mult))
                    did(V.tensor_copy(kinds[:, :, 0, :], r.oh1[:, :, :]))
                    did(V.tensor_tensor(kinds[:, :, 1, :], r.oh2[:, :, :], r.oh1[:, :, :], ALU.subtract))
                    did(V.tensor_tensor(kinds[:, :, 2, :], r.oh1[:, :, :], over(r.w1[:, :]), ALU.mult))
                    did(V.tensor_tensor(kinds[:, :, 3, :], r.oh2[:, :, :], over(r.w2[:, :]), ALU.mult))

        ex_done, ex_begun, a_made, masks_made = sem("ex_done"), sem("ex_begun"), sem("a_made"), sem("masks_made")
        pre_step = sem("pre_step")
        made, silu, mult, hid = sem("made"), sem("silu"), sem("mult"), sem("hid")
        used = [sem("used0"), sem("used1"), sem("used2")]
        z_made, z_split, o_made, y_done = sem("z_made"), sem("z_split"), sem("o_made"), sem("y_done")
        y_out = [sem("y_out0"), sem("y_out1")]
        hi_step = sem("hi_step")

        with nc.Block() as block:
            @block.sync
            def _(sp):
                for t in range(2):
                    sp.sem_inc(y_out[t], 1)
                with sp.Fori(0, NB) as n:
                    for t in range(2):
                        sp.wait_ge(y_done, 2 * n + t + 2)
                        sp.dma_start(out[n, t * P:(t + 1) * P, :], Y[t][:, :]).then_inc(y_out[t], 16)
                for t in range(2):
                    sp.wait_ge(y_out[t], 16 * NB + 1)

            @block.gpsimd
            def _(pool):
                with pool.Fori(0, NB) as n:
                    pool.wait_ge(masks_made, n + 1)
                    pool.sem_inc(ex_begun, 1)
                    src = kinds[:, bass.ds(2 * n, 2), :, :].rearrange("p t k e -> p (t k e)").unsqueeze(2).to_broadcast([P, 2 * 4 * E, R])
                    nc.gpsimd.tensor_copy(EX[:, :, :, :, :].rearrange("p t k e r -> p (t k e) r"), src).then_inc(ex_done, 1)

            @block.tensor
            def _(pe):
                MM = nc.tensor.matmul

                passes = ((0, 0), (0, 1), (1, 0))

                with pe.Fori(0, NB) as n:
                    toks = bass.ds(n * CH, CH)
                    X = (g.XTh, g.XTl)
                    pe.wait_ge(mult, NI * n + 3)
                    for w in range(2):
                        for k in range(KF):
                            for i, (s, m) in enumerate(passes):
                                mm = MM(GU[0][:, w * CH:(w + 1) * CH], agu[s][:, w, k, :], X[m][:, k, toks],
                                        start=(k == 0 and i == 0), stop=(k == KF - 1 and i == 2))
                    mm.then_inc(a_made, 1)
                    pe.wait_ge(ex_done, n + 1)
                    for kind in range(4):
                        for t in range(2):
                            mm = nc.tensor.transpose(GU[1 + kind // 2][:, kind % 2 * CH + t * P:kind % 2 * CH + (t + 1) * P],
                                                     EX[:, t, kind, :, :].rearrange("p e r -> p (e r)"), g.ident[:, :])
                    mm.then_inc(masks_made, 1)

                    def base(f):
                        if f == 1 or f == 2:
                            pe.wait_ge(pre_step, 8 * n + 2 * f)
                        if f >= 4:
                            pe.wait_ge(mult, NI * n + NUM[2, f - 4] + 4)
                        b = GU[(f + 3) % 4]
                        for w, wt in enumerate((wg, wu)):
                            for k in range(KF):
                                for i, (s, m) in enumerate(passes):
                                    mm = MM(b[:, w * CH:(w + 1) * CH], wt[s][:, k, f * P:(f + 1) * P], X[m][:, k, toks],
                                            start=(w == 0 and k == 0 and i == 0), stop=(k == KF - 1 and i == 2),
                                            skip_group_check=True)
                        mm.then_inc(made, 1)

                    def slot(kind, f):
                        if f == 0:
                            pe.wait_ge(pre_step, 8 * n + 4 + 2 * kind)
                        pe.wait_ge(mult, NI * n + NUM[kind - 1, f] + 4)
                        b = GU[(f + 3) % 4]
                        for w in range(2):
                            for i, (s, m) in enumerate(passes):
                                mm = MM(b[:, w * CH:(w + 1) * CH], bgu[s][:, w, f * P:(f + 1) * P], M[kind - 1][m][:, w, :],
                                        start=False, stop=(i == 2), skip_group_check=True)
                        mm.then_inc(made, 1)

                    def down(f):
                        if f == 0:
                            pe.wait_ge(y_done, 2 * n + 1)
                        pe.wait_ge(hid, NI * n + NUM[0, f] + 2)
                        H = HS[0][f % 2]
                        for t in range(2):
                            for i, (s, m) in enumerate(passes):
                                mm = MM(O[t][:, :], H[s][:, t * P:(t + 1) * P], wd[m][:, f, :],
                                        start=(f == 0 and i == 0), stop=False, skip_group_check=True)
                        mm.then_inc(used[0], 1)

                    def z(kind, f):
                        if f == 0:
                            pe.wait_ge(z_split, n + 1)
                        pe.wait_ge(hid, NI * n + NUM[kind, f] + 2)
                        H = HS[kind][f % 2]
                        for i, (s, m) in enumerate(passes):
                            mm = MM(Z[kind - 1][:, 0:CH], ad[s][:, f, :], H[m][:, :],
                                    start=(f == 0 and i == 0), stop=(f == FT - 1 and i == 2))
                        mm.then_inc(used[kind], 1)

                    for i in range(FT + 3):
                        if i < FT:
                            base(i)
                        if 0 <= i - 1 < FT:
                            slot(1, i - 1)
                        if 0 <= i - 2 < FT:
                            slot(2, i - 2)
                        if 0 <= i - 1 < FT:
                            down(i - 1)
                        if 0 <= i - 2 < FT:
                            z(1, i - 2)
                        if 0 <= i - 3 < FT:
                            z(2, i - 3)
                    pe.wait_ge(z_split, n + 2)
                    for t in range(2):
                        for i, (s, m) in enumerate(passes):
                            mm = MM(O[t][:, :], zz[s][:, t * P:(t + 1) * P], bd[m][:, :], start=False, stop=(i == 2),
                                    skip_group_check=True)
                        mm.then_inc(o_made, 1)

            @block.scalar
            def _(act):
                with act.Fori(0, NB) as n:
                    for k, (kind, f) in enumerate(ITEMS):
                        act.wait_ge(mult, NI * n + k + 1)
                        act.wait_ge(made, NI * n + k + 1)
                        nc.scalar.activation(SG[k % 3][:, :], GU[(f + 3) % 4][:, 0:CH], ACT.Silu, scale=1.0 / WS).then_inc(silu, 1)

            @block.vector
            def _(dve):
                V = nc.vector
                dve.sem_inc(mult, 3)
                dve.sem_inc(hid, 1)
                dve.sem_inc(masks_made, 1)
                dve.sem_inc(z_split, 1)
                dve.sem_inc(y_done, 1)
                for u in used:
                    dve.sem_inc(u, 1)
                with dve.Fori(0, NB) as n:
                    def pre(k, ins):
                        ins.then_inc(pre_step, 1)

                    gu = lambda b: b[:, :].rearrange("p (w c) -> p w c", w=2)
                    dve.wait_ge(a_made, n + 1)
                    pre(1, V.tensor_scalar(al[0][:, :, :], gu(GU[0]), 1.0 / WS, None, ALU.mult))
                    dve.wait_ge(pre_step, 8 * n + 1)
                    pre(2, V.scalar_tensor_tensor(out=al[1][:, :, :], in0=gu(GU[0]), scalar=1.0 / WS, in1=al[0][:, :, :],
                                                  op0=ALU.mult, op1=ALU.subtract))
                    dve.wait_ge(masks_made, n + 2)
                    pre(3, V.tensor_copy(MK[:, :, :], gu(GU[1])))
                    pre(4, V.tensor_copy(MW[:, :, :], gu(GU[2])))
                    dve.wait_ge(pre_step, 8 * n + 4)
                    for i in range(2):
                        for h in range(2):
                            pre(5 + 2 * i + h, V.tensor_tensor(M[i][h][:, :, :], al[h][:, :, :],
                                                               MK[:, i, :].unsqueeze(1).to_broadcast([ER, 2, CH]), ALU.mult))
                    for k, (kind, f) in enumerate(ITEMS):
                        b = GU[(f + 3) % 4]
                        dve.wait_ge(silu, NI * n + k + 1)
                        dve.wait_ge(hid, NI * n + k + 1)
                        V.scalar_tensor_tensor(out=HF[:, :], in0=b[:, CH:2 * CH], scalar=1.0 / WS, in1=SG[k % 3][:, :],
                                               op0=ALU.mult, op1=ALU.mult).then_inc(mult, 1)
                        dve.wait_ge(mult, NI * n + k + 4)
                        dve.wait_ge(used[kind], FT * n + max(0, f - 1) + 1)
                        H = HS[kind][f % 2]
                        V.tensor_copy(H[0][:, :], HF[:, :]).then_inc(hi_step, 1)
                        dve.wait_ge(hi_step, (NI + 1) * n + k + 1)
                        V.tensor_tensor(H[1][:, :], HF[:, :], H[0][:, :], ALU.subtract).then_inc(hid, 1)
                    dve.wait_ge(used[2], FT * (n + 1) + 1)
                    V.tensor_tensor(ZZ[:, 0, :], Z[0][:, 0:CH], MW[:, 0, :], ALU.mult).then_inc(z_made, 1)
                    V.tensor_tensor(ZZ[:, 1, :], Z[1][:, 0:CH], MW[:, 1, :], ALU.mult).then_inc(z_made, 1)
                    dve.wait_ge(z_made, 3 * n + 2)
                    V.tensor_tensor(ZZ[:, 0, :], ZZ[:, 0, :], ZZ[:, 1, :], ALU.add).then_inc(z_made, 1)
                    dve.wait_ge(z_made, 3 * n + 3)
                    V.tensor_copy(zz[0][:, :], ZZ[:, 0, :]).then_inc(hi_step, 1)
                    dve.wait_ge(hi_step, (NI + 1) * (n + 1))
                    V.tensor_tensor(zz[1][:, :], ZZ[:, 0, :], zz[0][:, :], ALU.subtract).then_inc(z_split, 1)
                    for t in range(2):
                        dve.wait_ge(o_made, 2 * n + t + 1)
                        dve.wait_ge(y_out[t], 16 * n + 1)
                        V.scalar_tensor_tensor(out=Y[t][:, :], in0=O[t][:, :], scalar=1.0 / WS, in1=g.x1[:, 2 * n + t, :],
                                               op0=ALU.mult, op1=ALU.add).then_inc(y_done, 1)


class Lasting:
    pass


def build(nc, ins, consts, out):
    with ExitStack() as ctx:
        sb = lambda name, shape, dt: ctx.enter_context(nc.sbuf_tensor(name, shape, dt))
        sem = lambda name: ctx.enter_context(nc.semaphore(name))
        g = Lasting()
        g.ident = sb("ident", [P, P], F32)
        g.x1 = sb("x1", [P, NT, T0], F32)
        g.XTh = sb("XTh", [P, KF, NB * S0], F16)
        g.XTl = sb("XTl", [P, KF, NB * S0], F16)
        g.x1_in, g.ident_set = sem("x1_in"), sem("ident_set")
        with nc.Block() as block:
            @block.gpsimd
            def _(pool):
                nc.gpsimd.memset(g.ident[:, :], 0.0).then_inc(g.ident_set, 1)
                pool.wait_ge(g.ident_set, 1)
                nc.gpsimd.affine_select(out=g.ident[:, :], in_=g.ident[:, :], compare_op=ALU.not_equal, fill=1.0,
                                        base=0, pattern=[[-1, P]], channel_multiplier=1).then_inc(g.ident_set, 1)
        layer0_attention(nc, g, ins["x"], ins["cond_2048"], ins["L0_cond_Wq"], ins["L0_cond_Wo"], consts["sel0"])
        layer0_experts(nc, g, ins["L0_ffn_w_router"], ins["L0_ffn_w_gate"], ins["L0_ffn_w_up"],
                       ins["L0_ffn_w_down"], consts["desc"])
        layer1_attention(nc, g, ins["cond_2048"], ins["L1_cond_W_emb"], ins["L1_cond_b_emb"], ins["L1_cond_g_norm"],
                         ins["L1_cond_W_qkv"], ins["L1_cond_g_q"], ins["L1_cond_g_k"], ins["L1_cond_W_out"], consts["sel1"])
        layer1_experts(nc, g, *(ins["L1_ffn_" + n] for n in ("Wg", "Wu", "Wd", "Wr", "Ag", "Bg", "Au", "Bu", "Ad", "Bd")),
                       consts["desc"], out)


def selection(heads):
    import numpy as np
    s = np.zeros((heads, heads // 4, P), np.float32)
    for h in range(heads):
        s[(h % 2) * (heads // 2) + h // 2, h // 4, 32 * (h % 4):32 * (h % 4) + 32] = 1.0
    return s


def descending():
    import numpy as np
    return np.broadcast_to(np.arange(E, 0, -1, dtype=np.float32), (P, NT, E)).copy()


def kernel(**inputs):
    import numpy as _np
    import concourse.bacc as _bacc
    from concourse import mybir as _mybir
    from concourse.bass_utils import run_bass_kernel_spmd as _run

    nc = _bacc.Bacc("TRN2", target_bir_lowering=False, num_devices=1)
    arrays, ins, consts = {}, {}, {}
    for name in inputs:
        a = _np.ascontiguousarray(inputs[name])
        arrays["in_" + name] = a
        ins[name] = nc.dram_tensor("in_" + name, a.shape, _mybir.dt.from_np(a.dtype), kind="ExternalInput").ap()
    for name, a in {"sel0": selection(8), "sel1": selection(16), "desc": descending()}.items():
        arrays["const_" + name] = a
        consts[name] = nc.dram_tensor("const_" + name, a.shape, F32, kind="ExternalInput").ap()
    out = nc.dram_tensor("out", (NB, S0, T0), F32, kind="ExternalOutput").ap()
    build(nc, ins, consts, out)
    return _run(nc, [arrays], core_ids=[0]).results[0]["out"]
```
